# Optimizing a Trainium2 kernel written in Bass

```python
import numpy as np
import jax
import jax.numpy as jnp

def _softmax(x, axis=-1):
    return jax.nn.softmax(x, axis=axis)

def _gelu(x):
    return jax.nn.gelu(x, approximate=True)

def _silu(x):
    return jax.nn.silu(x)

def _sigmoid(x):
    return jax.nn.sigmoid(x)

def _layernorm(x, axis=-1, eps=1e-05):
    m = jnp.mean(x, axis=axis, keepdims=True)
    v = jnp.var(x, axis=axis, keepdims=True)
    return (x - m) / jnp.sqrt(v + eps)

def _scatter_add(tgt, idx, src, axis=0):
    return tgt.at[idx].add(src)

def _segment_sum(src, seg, n):
    return jax.ops.segment_sum(src, seg, n)
kernel_name = 'mk_gnn_preln_d1_gnn_r64_99591d'

def setup_inputs(seed: int=0):
    np.random.seed(seed)
    _w = jnp.asarray

    def _rec_inputs():
        import jax
        import jax.numpy as jnp
        _gk = jax.random.key(seed)
        x = -0.0003713 + 1 * jax.random.normal(jax.random.fold_in(_gk, 1), (100000, 256), jnp.float32)
        src = jax.random.randint(jax.random.fold_in(_gk, 2), (25000,), 0, 100000, jnp.int32)
        dst = jax.random.randint(jax.random.fold_in(_gk, 3), (25000,), 0, 100000, jnp.int32)
        _o = jnp.argsort(dst, stable=True)
        src = src[_o]
        dst = dst[_o]
        edge_type_16 = jax.random.randint(jax.random.fold_in(_gk, 12), (25000,), 0, 16, jnp.int32)
        return (x, src, dst, edge_type_16)
    x, src, dst, edge_type_16 = _rec_inputs()

    def _L0_gnn_setup():
        import jax, jax.numpy as jnp
        import numpy as np
        NUM_BLOCKS = 64

        def rgcn_layer(x, src, dst, edge_type, W, root, bias):
            N, d = x.shape
            xj = x[src]
            out0 = x @ root + bias

            def body(out, inputs):
                r, Wr = inputs
                mask = (edge_type == r).astype(x.dtype)
                s = jax.ops.segment_sum(xj * mask[:, None], dst, num_segments=N)
                cnt = jax.ops.segment_sum(mask, dst, num_segments=N)
                h = s / jnp.maximum(cnt, 1.0)[:, None]
                hb = h.reshape(N, NUM_BLOCKS, d // NUM_BLOCKS)
                out = out + jnp.einsum('nbi,bio->nbo', hb, Wr).reshape(N, d)
                return (out, None)
            R = W.shape[0]
            out, _ = jax.lax.scan(body, out0, (jnp.arange(R), W))
            return out
        key = jax.random.key(seed)
        ks = jax.random.split(key, 9)
        N, d, R, E = (50000, 256, 16, 12500)
        db = d // NUM_BLOCKS
        return {'node_emb': jax.random.normal(ks[0], (N, d), jnp.float32), 'edge_index': jax.random.randint(ks[1], (2, E), 0, N), 'edge_type': jax.random.randint(ks[2], (E,), 0, R), 'W1': jax.random.normal(ks[3], (R, NUM_BLOCKS, db, db), jnp.float32) * 0.1, 'root1': jax.random.normal(ks[4], (d, d), jnp.float32) * 0.05, 'bias1': jnp.zeros((d,), jnp.float32), 'W2': jax.random.normal(ks[5], (R, NUM_BLOCKS, db, db), jnp.float32) * 0.1, 'root2': jax.random.normal(ks[6], (d, d), jnp.float32) * 0.05, 'bias2': jnp.zeros((d,), jnp.float32)}
    _L0_gnn_all = _L0_gnn_setup()
    _L0_gnn_in = {k: v for k, v in _L0_gnn_all.items() if k in ('W1', 'root1', 'bias1', 'W2', 'root2', 'bias2')}
    del _L0_gnn_all
    return {'x': x, 'src': src, 'dst': dst, 'edge_type_16': edge_type_16, 'L0_gnn_W1': _L0_gnn_in['W1'], 'L0_gnn_root1': _L0_gnn_in['root1'], 'L0_gnn_bias1': _L0_gnn_in['bias1'], 'L0_gnn_W2': _L0_gnn_in['W2'], 'L0_gnn_root2': _L0_gnn_in['root2'], 'L0_gnn_bias2': _L0_gnn_in['bias2']}

def reference(x, src, dst, edge_type_16, L0_gnn_W1, L0_gnn_root1, L0_gnn_bias1, L0_gnn_W2, L0_gnn_root2, L0_gnn_bias2):
    import jax
    import jax.numpy as jnp

    def _L0_gnn_ref(node_emb, edge_index, edge_type, W1, root1, bias1, W2, root2, bias2):
        import jax, jax.numpy as jnp
        import numpy as np
        NUM_BLOCKS = 64

        def rgcn_layer(x, src, dst, edge_type, W, root, bias):
            N, d = x.shape
            xj = x[src]
            out0 = x @ root + bias

            def body(out, inputs):
                r, Wr = inputs
                mask = (edge_type == r).astype(x.dtype)
                s = jax.ops.segment_sum(xj * mask[:, None], dst, num_segments=N)
                cnt = jax.ops.segment_sum(mask, dst, num_segments=N)
                h = s / jnp.maximum(cnt, 1.0)[:, None]
                hb = h.reshape(N, NUM_BLOCKS, d // NUM_BLOCKS)
                out = out + jnp.einsum('nbi,bio->nbo', hb, Wr).reshape(N, d)
                return (out, None)
            R = W.shape[0]
            out, _ = jax.lax.scan(body, out0, (jnp.arange(R), W))
            return out
        src, dst = (edge_index[0], edge_index[1])
        x = jax.nn.relu(rgcn_layer(node_emb, src, dst, edge_type, W1, root1, bias1))
        x = rgcn_layer(x, src, dst, edge_type, W2, root2, bias2)
        return x
    edge_index = jnp.stack([src, dst])
    h = jnp.maximum(_layernorm(x, axis=-1), 0.0)
    x = x + _L0_gnn_ref(h, edge_index, edge_type_16, L0_gnn_W1, L0_gnn_root1, L0_gnn_bias1, L0_gnn_W2, L0_gnn_root2, L0_gnn_bias2)
    return x

_drawn_inputs = setup_inputs


def setup_inputs(seed=0):
    import zlib

    import numpy as np

    out = dict(_drawn_inputs(seed))
    spreads = {'L0_gnn_bias1': (0.0, 0.1), 'L0_gnn_bias2': (0.0, 0.1)}
    factors = {}
    for name, (base, spread) in spreads.items():
        noise = np.random.default_rng([zlib.crc32(name.encode()), seed]).standard_normal(out[name].shape)
        drawn = base * np.exp(spread * noise) if base else spread * noise
        out[name] = jnp.asarray(drawn.astype(out[name].dtype))
    for name, factor in factors.items():
        out[name] = (out[name] * factor).astype(out[name].dtype)
    return out
```

```python
import concourse.bass as bass
import numpy as np
from concourse import mybir
from contextlib import ExitStack

F32, BF16, I32 = mybir.dt.float32, mybir.dt.bfloat16, mybir.dt.int32
ACT, ALU, AX = mybir.ActivationFunctionType, mybir.AluOpType, mybir.AxisListType
P = 128
EPS = 1e-5


def build(nc, x, src, dst, edge_type, w1, root1, bias1, w2, root2, bias2, out):
    N, D = x.shape
    E = src.shape[0]
    R, B, DB, _ = w1.shape
    K = D // P
    Q = 4
    GROUP = Q * P
    COLS = -(-E // P)
    COLS += COLS % 2
    EP = COLS * P
    PAIRS = COLS // 2
    GROUPS = -(-N // GROUP)
    assert GROUPS == 2 * PAIRS and K == 2 and B * DB == D
    LAST_ROW = N - GROUP
    NO_NODE = 1 << 17
    NOT_LAST = 1 << 20
    assert N <= NO_NODE and NO_NODE + NOT_LAST < 1 << 24
    ZERO_ROW = EP
    TABLE = -(-N // P) * P
    W = B * DB * DB
    LN_SLOTS = Q + 2

    ctx = ExitStack()
    with ctx:
        def sb(name, shape, dt=F32):
            return ctx.enter_context(nc.sbuf_tensor(name, shape, dt))

        def sem(name):
            return ctx.enter_context(nc.semaphore(name))

        def scratch(name, shape, dt=F32):
            return nc.dram_tensor(name, shape, dt, kind="Internal").ap()

        dst_shifted = scratch("dst_shifted", [EP + 2])
        edge_kinds = scratch("edge_kinds", [5, EP])
        edge_rows = scratch("edge_rows", [2 * COLS, 2, P])
        last_edge_of = scratch("last_edge_of", [TABLE, 1], I32)
        p_src = scratch("p_src", [EP, D])
        sum1 = scratch("sum1", [EP + 1, D])
        sum2 = scratch("sum2", [EP, D])

        ident = sb("ident", [P, P])
        upper = sb("upper", [P, P])
        last_part = sb("last_part", [P, 1])
        ones = sb("ones", [P, P], BF16)
        relation_of_part = sb("relation_of_part", [P, 1])
        eps_col = sb("eps_col", [P, 1])
        root1_sb = sb("root1_sb", [P, K, D])
        root2_sb = sb("root2_sb", [P, K, D])
        bias1_col = sb("bias1_col", [P, K])
        bias1_row = sb("bias1_row", [P, D])
        bias2_parts = sb("bias2_parts", [P, D], BF16)
        w_parts = [sb(f"w{n}_parts", [P, W], BF16) for n in (1, 2)]
        dst_col = sb("dst_col", [P, 1 + 2 * COLS + 2])
        inv_col = sb("inv_col", [P, 2 * COLS + 2])
        src_col = sb("src_col", [P, 2 * COLS + 2], I32)
        out_col = sb("out_col", [P, COLS], I32)
        edge_col = sb("edge_col", [P, COLS], I32)
        dsti_col = sb("dsti_col", [P, COLS + 4], I32)
        x_sb = sb("x_sb", [P, 4, Q, D])
        bn = sb("bn", [P, LN_SLOTS, 6])
        mv = sb("mv", [P, LN_SLOTS, 2])
        std = sb("std", [P, LN_SLOTS])
        rstd = sb("rstd", [P, LN_SLOTS])
        hn = sb("hn", [P, Q, D])
        hT = sb("hT", [P, K, Q, P])
        o1T = sb("o1T", [P, K, Q, P])
        xe = sb("xe", [P, 2, D])
        hn_e = sb("hn_e", [P, 2, D])
        hTe = sb("hTe", [P, 2, K, P])
        psrc_out = sb("psrc_out", [P, 2, D])
        psrc_in = sb("psrc_in", [P, 2, D])
        sum1_in = sb("sum1_in", [P, 2, D])
        h_scaled = sb("h_scaled", [P, 2, D])
        rows = sb("rows", [P, 2, 2, P])
        dcols = sb("dcols", [P, 3])
        icols = sb("icols", [P, 2])
        same_dst = sb("same_dst", [P, 2, P])
        carried = sb("carried", [P, 2, P])
        onehot = sb("onehot", [P, 2, P], BF16)
        prod = sb("prod", [P, W])
        msg = sb("msg", [P, 2, D])
        sums = sb("sums", [P, 2, D])
        idx_src = sb("idx_src", [P, 2], I32)
        idx_out = sb("idx_out", [P, 2], I32)
        idx_edge = sb("idx_edge", [P, 2], I32)
        idx_sum = sb("idx_sum", [P, 2], I32)
        xd = sb("xd", [P, 2, 2, D])
        s1d = sb("s1d", [P, 2, 2, D])
        s2d = sb("s2d", [P, 2, 2, D])
        resid = sb("resid", [P, 2, 2, D])
        final = sb("final", [P, 2, 2, D])
        idx_xd = sb("idx_xd", [P, 2], I32)
        idx_fin = sb("idx_fin", [P, 2], I32)

        bank = [ctx.enter_context(nc.psum_tensor(f"bank{i}", [P, 512], F32)) for i in range(8)]
        XT, P1, OUT, WX = bank[0:2], bank[2:4], bank[4:6], bank[6:8]

        turn = {e: sem(f"turn_{e}") for e in ("sp", "pool", "dve", "act", "pe")}

        def waits(eng, name, *pairs):
            some = False
            for s, n in pairs:
                if not (isinstance(n, int) and n <= 0):
                    eng.wait_ge(s, n)
                    some = True
            if some:
                eng.sem_inc(turn[name], 1)

        NB = EP // P
        FULL = E // NB
        REST = E - FULL * NB
        with ExitStack() as setup:
            def tb(name, shape, dt=F32):
                return setup.enter_context(nc.sbuf_tensor(name, shape, dt))

            raw = tb("raw", [P, 3, NB], I32)
            kinds = tb("kinds", [P, 5, NB])
            near = tb("near", [P, 2, NB])
            same = tb("same", [P, 2, NB])
            local = tb("local", [P, R, NB])
            onehot_s = tb("onehot_s", [P, R, NB])
            same_rep = tb("same_rep", [P, R, NB])
            run = tb("run", [P, NB])
            count = tb("count", [P, R, NB])
            relation_i = tb("relation_i", [P, R], I32)
            relation_f = tb("relation_f", [P, R])
            end_run = tb("end_run", [P, 2, R])
            carry_t = tb("carry_t", [R, 3, P])
            carry = tb("carry", [P, R])
            minus = tb("minus", [1, 2])
            table0 = tb("table0", [P, TABLE // P], I32)
            zero_row = tb("zero_row", [1, D])
            kind_rows = tb("kind_rows", [P, 2, 5, P])
            part_i = tb("part_i", [P, 1], I32)
            w_f = [tb(f"w{n}_f", [P, W]) for n in (1, 2)]
            w_r = tb("w_r", [P, W])
            b2_f = tb("b2_f", [P, D])
            w_low = tb("w_low", [P, 2, W], BF16)
            back = tb("back", [P, 1])
            flag_row = tb("flag_row", [1, 1])
            flag = tb("flag", [1, 1], I32)
            place = tb("place", [P, R * NB], I32)
            edge_i = tb("edge_i", [P, NB], I32)
            edge_f = tb("edge_f", [P, NB])
            rank = tb("rank", [P, NB])
            rank_i = tb("rank_i", [P, NB], I32)
            of_edge = tb("of_edge", [P, 4])
            rank_col = tb("rank_col", [P, 1], I32)
            payload = tb("payload", [P, 4], I32)
            sorted_in = tb("sorted_in", [P, NB, 4], I32)
            sorted_edges = scratch("sorted_edges", [EP, 4], I32)

            padded = sem("padded")
            edges_in = sem("edges_in")
            consts_in = sem("consts_in")
            pool_consts = sem("pool_consts")
            dst_out = sem("dst_out")
            near_in = sem("near_in")
            kinds_ready = sem("kinds_ready")
            kinds_out = sem("kinds_out")
            kind_rows_in = sem("kind_rows_in")
            rows_out = sem("rows_out")
            table_out = sem("table_out")
            v = sem("setup_dve_step")
            t_done = sem("setup_transposed")
            cols_ready = sem("cols_ready")
            back_ready, back_turned, flag_ready = sem("back_ready"), sem("back_turned"), sem("flag_ready")
            chunk_in, chunk_used = sem("chunk_in"), sem("chunk_used")
            cols_taken, compared, counted, ranked = sem("cols_taken"), sem("compared"), sem("counted"), sem("ranked")
            rank_ready, staged, moved = sem("rank_ready"), sem("staged"), sem("moved")
            all_moved, sorted_ready, unpacked = sem("all_moved"), sem("sorted_ready"), sem("unpacked")
            dst_out2, near_in2 = sem("dst_out2"), sem("near_in2")
            CHUNK = R * NB
            CHUNKS = EP // CHUNK
            assert CHUNKS * CHUNK == EP

            with nc.Block() as block:
                @block.sync
                def _(sp):
                    sp.wait_ge(padded, 1)
                    for k, a in enumerate((dst, edge_type, src)):
                        sp.dma_start(raw[0:FULL, k, :], a[0:FULL * NB].rearrange("(p c) -> p c", c=NB)).then_inc(edges_in, 16)
                        sp.dma_start(raw[FULL:FULL + 1, k, 0:REST], a[FULL * NB:E].rearrange("(p c) -> p c", p=1)).then_inc(edges_in, 16)
                    sp.wait_ge(padded, 2)
                    for n, w in enumerate((w1, w2)):
                        for q in range(3):
                            sp.dma_start(w_f[n][32 * q:32 * q + R, :], w.rearrange("r b i o -> r (b i o)")).then_inc(consts_in, 16)
                    for q in range(3):
                        sp.dma_start(b2_f[32 * q:32 * q + 1, :], bias2.rearrange("(a d) -> a d", a=1)).then_inc(consts_in, 16)
                    sp.dma_start(root1_sb[:, :, :], root1.rearrange("(k p) d -> p k d", p=P)).then_inc(consts_in, 16)
                    sp.dma_start(root2_sb[:, :, :], root2.rearrange("(k p) d -> p k d", p=P)).then_inc(consts_in, 16)
                    with nc.allow_non_contiguous_dma(reason="one column per feature chunk"):
                        sp.dma_start(bias1_col[:, :], bias1.rearrange("(k p) -> p k", p=P)).then_inc(consts_in, 16)
                    sp.dma_start(bias1_row[:, :], bias1.partition_broadcast(P)).then_inc(consts_in, 16)
                    sp.wait_ge(kinds_ready, 1)
                    sp.dma_start(dst_shifted[1:EP + 1].rearrange("(p c) -> p c", c=NB), kinds[:, 0, :]).then_inc(dst_out, 16)
                    sp.dma_start(dst_shifted[0:1].rearrange("(p c) -> p c", p=1), minus[:, 0:1]).then_inc(dst_out, 16)
                    sp.dma_start(dst_shifted[EP + 1:EP + 2].rearrange("(p c) -> p c", p=1), minus[:, 1:2]).then_inc(dst_out, 16)
                    sp.wait_ge(dst_out, 48)
                    for k in range(2):
                        sp.dma_start(near[:, k, :], dst_shifted[2 * k:2 * k + EP].rearrange("(p c) -> p c", c=NB)).then_inc(near_in, 16)
                    sp.wait_ge(flag_ready, 1)
                    unsorted = sp.value_load(flag[0:1, 0:1], min_val=0, max_val=1)
                    with sp.If(unsorted > 0):
                        for n in range(CHUNKS):
                            sp.wait_ge(chunk_used, n)
                            sp.dma_start(local[:, :, :].rearrange("p r c -> p (r c)"),
                                         dst_shifted[1 + n * CHUNK:1 + (n + 1) * CHUNK].partition_broadcast(P)).then_inc(chunk_in, 16)
                        sp.wait_ge(all_moved, 1)
                        sp.dma_start(sorted_in[:, :, :], sorted_edges.rearrange("(p c) k -> p c k", c=NB)).then_inc(sorted_ready, 16)
                        sp.wait_ge(unpacked, 1)
                        sp.dma_start(dst_shifted[1:EP + 1].rearrange("(p c) -> p c", c=NB), kinds[:, 0, :]).then_inc(dst_out2, 16)
                        sp.wait_ge(dst_out2, 16)
                        for k in range(2):
                            sp.dma_start(near[:, k, :], dst_shifted[2 * k:2 * k + EP].rearrange("(p c) -> p c", c=NB)).then_inc(near_in2, 16)
                    sp.wait_ge(kinds_ready, 2)
                    sp.dma_start(edge_kinds.rearrange("k (p c) -> p k c", c=NB), kinds[:, :, :]).then_inc(kinds_out, 16)
                    sp.wait_ge(kinds_out, 16)
                    by_tile = edge_kinds.rearrange("k (c p) -> c k p", p=P)
                    sp.dma_start(kind_rows[:, 0, :, :], by_tile[0:P]).then_inc(kind_rows_in, 16)
                    sp.dma_start(kind_rows[0:COLS - P, 1, :, :], by_tile[P:COLS]).then_inc(kind_rows_in, 16)
                    sp.wait_ge(kind_rows_in, 32)
                    for again in (0, COLS):
                        sp.dma_start(edge_rows[again:again + P], kind_rows[:, 0, 0:2, :]).then_inc(rows_out, 16)
                        sp.dma_start(edge_rows[again + P:again + COLS], kind_rows[0:COLS - P, 1, 0:2, :]).then_inc(rows_out, 16)
                    sp.wait_ge(pool_consts, 1)
                    sp.dma_start(last_edge_of.rearrange("(p c) a -> p (c a)", p=P), table0[:, :]).then_inc(table_out, 16)
                    sp.dma_start(sum1[ZERO_ROW:ZERO_ROW + 1, :], zero_row[:, :]).then_inc(table_out, 16)
                    sp.wait_ge(rows_out, 64)
                    sp.wait_ge(table_out, 32)
                    sp.wait_ge(consts_in, 13 * 16)

                @block.gpsimd
                def _(pool):
                    pool.memset(ident[:, :], 0.0).then_inc(turn["pool"], 1)
                    pool.memset(upper[:, :], 1.0).then_inc(turn["pool"], 1)
                    pool.memset(table0[:, :], ZERO_ROW)
                    pool.memset(zero_row[:, :], 0.0)
                    pool.iota(relation_i[:, :], pattern=[[1, R]], base=0, channel_multiplier=0)
                    pool.iota(edge_col[:, :], pattern=[[P, COLS]], base=0, channel_multiplier=1)
                    pool.iota(part_i[:, :], pattern=[[0, 1]], base=0, channel_multiplier=1)
                    pool.iota(place[:, :], pattern=[[1, R * NB]], base=0, channel_multiplier=0)
                    pool.iota(edge_i[:, :], pattern=[[1, NB]], base=0, channel_multiplier=NB)
                    pool.memset(payload[:, :], 0)
                    pool.wait_ge(turn["pool"], 2)
                    pool.affine_select(out=ident[:, :], in_=ident[:, :], compare_op=ALU.not_equal, fill=1.0,
                                       base=0, pattern=[[-1, P]], channel_multiplier=1)
                    pool.affine_select(out=upper[:, :], in_=upper[:, :], compare_op=ALU.is_ge, fill=0.0,
                                       base=0, pattern=[[1, P]], channel_multiplier=-1).then_inc(pool_consts, 1)
                    pool.wait_ge(flag_ready, 1)
                    unsorted = pool.value_load(flag[0:1, 0:1], min_val=0, max_val=1)
                    with pool.If(unsorted > 0):
                        pool.wait_ge(rank_ready, 1)
                        with pool.Fori(0, NB) as c:
                            waits(pool, "pool", (moved, 16 * c))
                            nc.gpsimd.tensor_copy(rank_col[:, :], rank_i[:, bass.ds(c, 1)])
                            nc.gpsimd.tensor_copy(payload[:, 0:3].unsqueeze(2), raw[:, :, bass.ds(c, 1)]).then_inc(staged, 1)
                            waits(pool, "pool", (staged, c + 1))
                            pool.indirect_dma_start(out=sorted_edges, out_offset=bass.IndirectOffsetOnAxis(ap=rank_col[:, :], axis=0),
                                                    in_=payload[:, :], in_offset=None).then_inc(moved, 16)
                        waits(pool, "pool", (moved, 16 * NB))
                        pool.sem_inc(all_moved, 1)

                @block.vector
                def _(dve):
                    step = [0]

                    def do(ins):
                        step[0] += 1
                        ins.then_inc(v, 1)

                    def settle():
                        dve.wait_ge(v, step[0])

                    V = nc.vector
                    do(V.memset(raw[:, 0, :], NO_NODE))
                    settle()
                    V.memset(raw[:, 1:3, :], 0).then_inc(padded, 1)
                    for t in (*w_f, b2_f):
                        do(V.memset(t[:, :], 0.0))
                    do(V.memset(minus[:, :], -1.0))
                    do(V.memset(eps_col[:, :], EPS))
                    do(V.memset(ones[:, :], 1.0))
                    do(V.memset(mv[:, :, :], 1.0))
                    do(V.memset(bn[:, :, :], 1.0))
                    do(V.memset(sums[:, :, :], 0.0))
                    do(V.memset(xd[:, :, :, :], 0.0))
                    do(V.memset(dst_col[:, :], -1.0))
                    do(V.memset(inv_col[:, :], 1.0))
                    do(V.memset(src_col[:, :], 0))
                    do(V.memset(dsti_col[:, :], 0))
                    settle()
                    dve.sem_inc(padded, 1)
                    dve.wait_ge(edges_in, 96)
                    do(V.tensor_copy(kinds[:, 0:3, :], raw[:, :, :]))
                    settle()
                    dve.sem_inc(kinds_ready, 1)
                    dve.wait_ge(pool_consts, 1)
                    do(V.tensor_copy(relation_f[:, :], relation_i[:, :]))
                    for q in range(4):
                        do(V.tensor_scalar(relation_of_part[32 * q:32 * q + 32, :], part_i[32 * q:32 * q + 32, :],
                                           float(-32 * q), None, ALU.add))
                    do(V.tensor_copy(last_part[:, :], ident[:, P - 1:P]))
                    settle()
                    dve.wait_ge(near_in, 32)
                    do(V.tensor_tensor(same[:, 0, :], kinds[:, 0, :], near[:, 0, :], op=ALU.is_lt))
                    settle()
                    do(V.tensor_reduce(out=back[:, :], in_=same[:, 0, :], axis=AX.X, op=ALU.max))
                    settle()
                    dve.sem_inc(back_ready, 1)
                    dve.wait_ge(back_turned, 1)
                    do(V.tensor_reduce(out=flag_row[:, :], in_=bank[1][0:1, 0:P], axis=AX.X, op=ALU.max))
                    settle()
                    do(V.tensor_copy(flag[:, :], flag_row[:, :]))
                    do(V.tensor_copy(edge_f[:, :], edge_i[:, :]))
                    do(V.memset(rank[:, :], 0.0))
                    settle()
                    dve.sem_inc(flag_ready, 1)
                    unsorted = dve.value_load(flag[0:1, 0:1], min_val=0, max_val=1)
                    with dve.If(unsorted > 0):
                        for n in range(CHUNKS):
                            dve.wait_ge(chunk_in, 16 * (n + 1))
                            with dve.Fori(0, NB) as c:
                                t = c + n * NB
                                waits(dve, "dve", (counted, t), (ranked, t))
                                V.tensor_copy(of_edge[:, 0:1], kinds[:, 0, bass.ds(c, 1)])
                                V.tensor_scalar(of_edge[:, 1:2], edge_f[:, bass.ds(c, 1)], float(-n * CHUNK), None,
                                                ALU.add).then_inc(cols_taken, 1)
                                waits(dve, "dve", (cols_taken, t + 1))
                                low = onehot_s[:, :, :].rearrange("p r c -> p (r c)")
                                equal = same_rep[:, :, :].rearrange("p r c -> p (r c)")
                                before = count[:, :, :].rearrange("p r c -> p (r c)")
                                dsts = local[:, :, :].rearrange("p r c -> p (r c)")
                                V.tensor_scalar(low, dsts, of_edge[:, 0:1], None, ALU.is_lt)
                                V.tensor_scalar(equal, dsts, of_edge[:, 0:1], None, ALU.is_equal).then_inc(compared, 1)
                                waits(dve, "dve", (compared, 2 * t + 1))
                                V.scalar_tensor_tensor(out=before, in0=place[:, :], scalar=of_edge[:, 1:2], in1=equal,
                                                       op0=ALU.is_lt, op1=ALU.mult).then_inc(compared, 1)
                                waits(dve, "dve", (compared, 2 * t + 2))
                                V.tensor_reduce(out=of_edge[:, 2:3], in_=low, axis=AX.X, op=ALU.add)
                                V.tensor_reduce(out=of_edge[:, 3:4], in_=before, axis=AX.X, op=ALU.add).then_inc(counted, 1)
                                waits(dve, "dve", (counted, t + 1))
                                V.scalar_tensor_tensor(out=rank[:, bass.ds(c, 1)], in0=of_edge[:, 2:3], scalar=of_edge[:, 3:4],
                                                       in1=rank[:, bass.ds(c, 1)], op0=ALU.add, op1=ALU.add).then_inc(ranked, 1)
                            waits(dve, "dve", (ranked, NB * (n + 1)))
                            dve.sem_inc(chunk_used, 1)
                        V.tensor_copy(rank_i[:, :], rank[:, :]).then_inc(rank_ready, 1)
                        dve.wait_ge(sorted_ready, 16)
                        V.tensor_copy(kinds[:, 0:3, :], sorted_in[:, :, 0:3].rearrange("p c k -> p k c")).then_inc(unpacked, 1)
                        dve.wait_ge(near_in2, 32)
                    do(V.tensor_tensor(onehot_s[:, :, :], kinds[:, 1:2, :].broadcast_to([P, R, NB]),
                                       relation_f[:, :].unsqueeze(2).broadcast_to([P, R, NB]), op=ALU.is_equal))
                    for k in range(2):
                        do(V.tensor_tensor(same[:, k, :], kinds[:, 0, :], near[:, k, :], op=ALU.is_equal))
                    settle()
                    do(V.scalar_tensor_tensor(out=kinds[:, 4, :], in0=same[:, 1, :], scalar=float(NOT_LAST),
                                              in1=kinds[:, 0, :], op0=ALU.mult, op1=ALU.add))
                    for k in range(2):
                        def way(t):
                            return t if k == 0 else t[:, ::-1]
                        first = 0 if k == 0 else NB - 1
                        do(V.tensor_copy(same_rep[:, :, :], same[:, k:k + 1, :].broadcast_to([P, R, NB])))
                        settle()
                        do(V.memset(same_rep[:, :, first:first + 1], 0.0))
                        do(V.tensor_tensor_scan(way(run[:, :]), way(same[:, k, :]), way(same[:, k, :]), 1.0,
                                                op0=ALU.mult, op1=ALU.min))
                        settle()
                        do(V.tensor_tensor_scan(way(local[:, :, :].rearrange("p r c -> p (r c)")),
                                                way(same_rep[:, :, :].rearrange("p r c -> p (r c)")),
                                                way(onehot_s[:, :, :].rearrange("p r c -> p (r c)")), 0.0,
                                                op0=ALU.mult, op1=ALU.add))
                        settle()
                        end = NB - 1 - first
                        do(V.tensor_copy(end_run[:, 0, :], local[:, :, end]))
                        do(V.tensor_copy(end_run[:, 1, :], run[:, end:end + 1].broadcast_to([P, R])))
                        settle()
                        dve.sem_inc(cols_ready, 1)
                        dve.wait_ge(t_done, 1 + 2 * k)
                        do(V.tensor_copy(carry_t[:, 0:2, :], bank[0][0:R, 0:2 * P].rearrange("r (a p) -> r a p", a=2)))
                        settle()
                        do(V.memset(carry_t[:, 2, :], 0.0))
                        settle()
                        if k == 0:
                            do(V.tensor_tensor_scan(carry_t[:, 2, 1:P], carry_t[:, 1, 0:P - 1], carry_t[:, 0, 0:P - 1], 0.0,
                                                    op0=ALU.mult, op1=ALU.add))
                        else:
                            do(V.tensor_tensor_scan(carry_t[:, 2, 0:P - 1][:, ::-1], carry_t[:, 1, 1:P][:, ::-1],
                                                    carry_t[:, 0, 1:P][:, ::-1], 0.0, op0=ALU.mult, op1=ALU.add))
                        settle()
                        dve.sem_inc(cols_ready, 1)
                        dve.wait_ge(t_done, 2 + 2 * k)
                        do(V.tensor_copy(carry[:, :], bank[0][:, 256:256 + R]))
                        settle()
                        do(V.tensor_tensor(same_rep[:, :, :], run[:, :].unsqueeze(1).broadcast_to([P, R, NB]),
                                           carry[:, :].unsqueeze(2).broadcast_to([P, R, NB]), op=ALU.mult))
                        settle()
                        if k == 0:
                            do(V.tensor_tensor(count[:, :, :], local[:, :, :], same_rep[:, :, :], op=ALU.add))
                        else:
                            do(V.tensor_tensor(local[:, :, :], local[:, :, :], same_rep[:, :, :], op=ALU.add))
                            settle()
                            do(V.tensor_tensor(count[:, :, :], count[:, :, :], local[:, :, :], op=ALU.add))
                        settle()
                    do(V.tensor_tensor(count[:, :, :], count[:, :, :], onehot_s[:, :, :], op=ALU.mult))
                    settle()
                    do(V.tensor_reduce(out=run[:, :], in_=count[:, :, :].rearrange("p r c -> p c r"), axis=AX.X, op=ALU.add))
                    settle()
                    do(V.tensor_scalar(run[:, :], run[:, :], -1.0, 1.0, ALU.add, ALU.max))
                    settle()
                    do(V.reciprocal(kinds[:, 3, :], run[:, :]))
                    settle()
                    dve.sem_inc(kinds_ready, 1)
                    dve.wait_ge(consts_in, 13 * 16)
                    for dest, whole, n in ((w_parts[0], w_f[0], W), (w_parts[1], w_f[1], W), (bias2_parts, b2_f, D)):
                        part = w_low[:, :, 0:n]
                        do(V.memset(dest[:, :], 0.0))
                        if n == W:
                            do(V.tensor_copy(w_r[:, 0:n].rearrange("p (b o i) -> p b o i", o=DB, i=DB),
                                             whole[:, :].rearrange("p (b i o) -> p b o i", o=DB, i=DB)))
                        else:
                            do(V.tensor_copy(w_r[:, 0:n], whole[:, :]))
                        settle()
                        do(V.tensor_copy(dest[:, :], w_r[:, 0:n]))
                        settle()
                        do(V.tensor_tensor(w_r[:, 0:n], w_r[:, 0:n], dest[:, :], op=ALU.subtract))
                        settle()
                        do(V.tensor_copy(part[:, 0, :], w_r[:, 0:n]))
                        settle()
                        do(V.tensor_tensor(w_r[:, 0:n], w_r[:, 0:n], part[:, 0, :], op=ALU.subtract))
                        do(V.tensor_copy(dest[32:64, :], part[32:64, 0, :]))
                        settle()
                        do(V.tensor_copy(dest[64:96, :], w_r[64:96, 0:n]))
                        do(V.memset(dest[96:128, :], 0.0))
                        settle()
                    dve.wait_ge(t_done, 5)
                    kind_at = lambda s: bank[2 + s // 2][:, (s % 2) * 256:(s % 2) * 256 + COLS]
                    for again in (0, COLS):
                        do(V.tensor_copy(dst_col[:, 1 + again:1 + again + COLS], kind_at(0)))
                        do(V.tensor_copy(src_col[:, again:again + COLS], kind_at(1)))
                        do(V.tensor_copy(inv_col[:, again:again + COLS], kind_at(2)))
                    do(V.tensor_copy(out_col[:, :], kind_at(3)))
                    do(V.tensor_copy(dsti_col[:, 0:COLS], kind_at(0)))
                    settle()

                @block.tensor
                def _(pe):
                    T = nc.tensor.transpose
                    pe.wait_ge(pool_consts, 1)
                    pe.wait_ge(back_ready, 1)
                    T(bank[1][0:1, 0:P], back[:, :], ident[:, :]).then_inc(back_turned, 1)
                    for k in range(2):
                        pe.wait_ge(cols_ready, 1 + 2 * k)
                        T(bank[0][0:R, 0:P], end_run[:, 0, :], ident[:, :])
                        T(bank[0][0:R, P:2 * P], end_run[:, 1, :], ident[:, :]).then_inc(t_done, 1)
                        pe.wait_ge(cols_ready, 2 + 2 * k)
                        T(bank[0][:, 256:256 + R], carry_t[:, 2, :], ident[0:R, 0:R]).then_inc(t_done, 1)
                    pe.wait_ge(kind_rows_in, 32)
                    for s, k in enumerate((0, 2, 3, 4)):
                        at = (s % 2) * 256
                        T(bank[2 + s // 2][:, at:at + P], kind_rows[:, 0, k, :], ident[:, :])
                        last = T(bank[2 + s // 2][:, at + P:at + COLS], kind_rows[0:COLS - P, 1, k, :],
                                 ident[0:COLS - P, 0:COLS - P])
                    last.then_inc(t_done, 1)

        x_loaded, x_stored = sem("x_loaded"), sem("x_stored")
        stats_ready, std_ready, rstd_ready = sem("stats_ready"), sem("std_ready"), sem("rstd_ready")
        bn_done = sem("bn_done")
        hn_ready, xT_done, hT_ready = sem("hn_ready"), sem("xT_done"), sem("hT_ready")
        mm1_done, o1_ready, mm2_done, res_ready = sem("mm1_done"), sem("o1_ready"), sem("mm2_done"), sem("res_ready")
        rows_loaded, cols_read, masks_ready = sem("rows_loaded"), sem("cols_read"), sem("masks_ready")
        xe_gathered, table_scattered, idx_ready = sem("xe_gathered"), sem("table_scattered"), sem("idx_ready")
        edge_rows_ready, h_ready = sem("edge_rows_ready"), sem("h_ready")
        eT_done, hTe_ready, eP_done, psrc_ready = sem("eT_done"), sem("hTe_ready"), sem("eP_done"), sem("psrc_ready")
        psrc_stored, psrc_loaded = sem("psrc_stored"), sem("psrc_loaded")
        wexp_done, prod_done, msg_ready = sem("wexp_done"), sem("prod_done"), sem("msg_ready")
        agg_done, sums_ready, sums_stored = sem("agg_done"), sem("sums_ready"), sem("sums_stored")
        table_read, idx2_ready, sum1_gathered = sem("table_read"), sem("idx2_ready"), sem("sum1_gathered")

        LOOKAHEAD = 3
        PEEL = GROUPS - LOOKAHEAD - 1

        def nodes_of(t, g):
            start = g * GROUP if not isinstance(g, int) else min(g * GROUP, LAST_ROW)
            return t[bass.ds(start, GROUP), :].rearrange("(p q) d -> p q d", q=Q)

        def slot(g):
            return x_sb[:, bass.ds(g % 4, 1), :, :].rearrange("p a q d -> p (a q) d")

        def pair_rows(t, pair):
            return t[bass.ds(pair * 2 * P, 2 * P), :].rearrange("(u p) d -> p u d", p=P)

        def both_loops(eng, step):
            with eng.Fori(0, PAIRS) as g:
                step(g, 1)
            with eng.Fori(PAIRS, PEEL) as g:
                step(g, 2)
            for g in range(PEEL, GROUPS):
                step(g, 2)

        with nc.Block() as block:
            @block.sync
            def _(sp):
                def load_x(g):
                    sp.dma_start(slot(g), nodes_of(x, g)).then_inc(x_loaded, 16)

                def load_rows(g):
                    sp.dma_start(rows[:, :, :, :].rearrange("p u k e -> p (u k e)"),
                                 edge_rows[bass.ds(2 * g, 2)].rearrange("u k e -> (u k e)").partition_broadcast(P)
                                 ).then_inc(rows_loaded, 16)

                def load_psrc(pair):
                    sp.dma_start(psrc_in[:, :, :], pair_rows(p_src, pair)).then_inc(psrc_loaded, 16)

                for g in range(LOOKAHEAD):
                    load_x(g)
                    waits(sp, "sp", (x_loaded, 16 * (g + 1)))
                load_rows(0)

                def step(g, layer):
                    known = isinstance(g, int)
                    if not known or g + LOOKAHEAD < GROUPS:
                        waits(sp, "sp", (x_stored, 16 * g), (x_loaded, 16 * (g + LOOKAHEAD)))
                        load_x(g + LOOKAHEAD)
                    if not known or g + 1 < GROUPS:
                        waits(sp, "sp", (masks_ready, g + 1))
                        load_rows(g + 1)
                    if layer == 2 and (not known or g + 1 < GROUPS):
                        waits(sp, "sp", (edge_rows_ready, g + 1))
                        load_psrc(g + 1 - PAIRS)
                    if known and g == GROUPS - 1:
                        waits(sp, "sp", (x_stored, 16 * g))
                    waits(sp, "sp", (res_ready, 2 * g + 2))
                    sp.dma_start(nodes_of(out, g), slot(g)).then_inc(x_stored, 16)
                    if layer == 1:
                        waits(sp, "sp", (psrc_ready, g + 1))
                        sp.dma_start(pair_rows(p_src, g), psrc_out[:, :, :]).then_inc(psrc_stored, 16)
                    waits(sp, "sp", (sums_ready, 2 * g + 2))
                    sp.dma_start(pair_rows(sum1 if layer == 1 else sum2, g if layer == 1 else g - PAIRS),
                                 sums[:, :, :]).then_inc(sums_stored, 16)

                with sp.Fori(0, PAIRS) as g:
                    step(g, 1)
                waits(sp, "sp", (psrc_stored, 16 * PAIRS))
                load_psrc(0)
                with sp.Fori(PAIRS, PEEL) as g:
                    step(g, 2)
                for g in range(PEEL, GROUPS):
                    step(g, 2)
                waits(sp, "sp", (x_stored, 16 * GROUPS), (sums_stored, 16 * GROUPS))

            @block.gpsimd
            def _(pool):
                def at(ap):
                    return bass.IndirectOffsetOnAxis(ap=ap, axis=0)

                def gather_x(g):
                    waits(pool, "pool", (xe_gathered, 32 * g))
                    nc.gpsimd.tensor_copy(idx_src[:, :], src_col[:, bass.ds(2 * g, 2)]).then_inc(idx_ready, 1)

                gather_x(0)
                waits(pool, "pool", (idx_ready, 1))
                for u in range(2):
                    pool.indirect_dma_start(out=xe[:, u, :], out_offset=None, in_=x,
                                            in_offset=at(idx_src[:, u:u + 1])).then_inc(xe_gathered, 16)

                with pool.Fori(0, PAIRS) as g:
                    gather_x(g + 1)
                    waits(pool, "pool", (table_scattered, 32 * g))
                    nc.gpsimd.tensor_copy(idx_out[:, :], out_col[:, bass.ds(2 * g, 2)]).then_inc(idx_ready, 1)
                    nc.gpsimd.tensor_copy(idx_edge[:, :], edge_col[:, bass.ds(2 * g, 2)]).then_inc(idx_ready, 1)
                    waits(pool, "pool", (idx_ready, 3 * g + 4))
                    for u in range(2):
                        pool.indirect_dma_start(out=last_edge_of, out_offset=at(idx_out[:, u:u + 1]),
                                                in_=idx_edge[:, u:u + 1], in_offset=None,
                                                bounds_check=N - 1, oob_is_err=False).then_inc(table_scattered, 16)
                    waits(pool, "pool", (edge_rows_ready, g + 1))
                    for u in range(2):
                        pool.indirect_dma_start(out=xe[:, u, :], out_offset=None, in_=x,
                                                in_offset=at(idx_src[:, u:u + 1])).then_inc(xe_gathered, 16)

                def gather_sum1(g):
                    n = g - PAIRS
                    waits(pool, "pool", (table_read, 32 * n), (sum1_gathered, 32 * n))
                    nc.gpsimd.tensor_copy(idx_src[:, :], src_col[:, bass.ds(2 * g, 2)]).then_inc(idx2_ready, 1)
                    waits(pool, "pool", (idx2_ready, n + 1))
                    for u in range(2):
                        pool.indirect_dma_start(out=idx_sum[:, u:u + 1], out_offset=None, in_=last_edge_of,
                                                in_offset=at(idx_src[:, u:u + 1])).then_inc(table_read, 16)
                    waits(pool, "pool", (table_read, 32 * n + 32), (edge_rows_ready, g))
                    for u in range(2):
                        pool.indirect_dma_start(out=sum1_in[:, u, :], out_offset=None, in_=sum1,
                                                in_offset=at(idx_sum[:, u:u + 1])).then_inc(sum1_gathered, 16)

                waits(pool, "pool", (table_scattered, 32 * PAIRS), (sums_stored, 16 * PAIRS), (xe_gathered, 32 * (PAIRS + 1)))
                gather_sum1(PAIRS)
                with pool.Fori(PAIRS + 1, GROUPS) as g:
                    gather_sum1(g)

            @block.vector
            def _(dve):
                V = nc.vector

                def stats(n, edges):
                    waits(dve, "dve", (hn_ready, n), (edge_rows_ready, n - 1), (std_ready, n),
                          (x_loaded, 16 * (n + 1)), *([(xe_gathered, 32 * n)] if edges else []))
                    if edges:
                        for u in range(2):
                            V.bn_stats(bn[:, Q + u, :], xe[:, u, :])
                    x_n = slot(n)
                    for q in range(Q):
                        last = V.bn_stats(bn[:, q, :], x_n[:, q, :])
                    last.then_inc(bn_done, 1)
                    waits(dve, "dve", (bn_done, n + 1))
                    for s in range(LN_SLOTS if edges else Q):
                        last = V.bn_aggr(mv[:, s, :], bn[:, s, :])
                    last.then_inc(stats_ready, 1)

                def root(n):
                    waits(dve, "dve", (std_ready, n + 1))
                    V.reciprocal(rstd[:, :], std[:, :]).then_inc(rstd_ready, 1)
                    waits(dve, "dve", (rstd_ready, n + 1))

                def normalise(o, i, s):
                    return V.tensor_scalar(o, i, mv[:, s, 0:1], rstd[:, s:s + 1], ALU.subtract, ALU.mult)

                def normalise_nodes(n):
                    waits(dve, "dve", (xT_done, n))
                    x_n = slot(n)
                    for q in range(Q):
                        last = normalise(hn[:, q, :], x_n[:, q, :], q)
                    last.then_inc(hn_ready, 1)

                def product(g, u, layer):
                    h = h_scaled[:, u, :].rearrange("p (b i) -> p b i", i=DB)
                    waits(dve, "dve", (wexp_done, 2 * g + u + 1), (h_ready, g + 1), (msg_ready, 2 * g + u))
                    for half in range(2):
                        b = slice(half * B // 2, (half + 1) * B // 2)
                        last = V.tensor_tensor(
                            prod[:, half * 512:half * 512 + 512].rearrange("p (b o i) -> p b o i", o=DB, i=DB),
                            WX[half][:, :].rearrange("p (b o i) -> p b o i", o=DB, i=DB),
                            h[:, b, :].unsqueeze(2).broadcast_to([P, B // 2, DB, DB]), op=ALU.mult)
                    last.then_inc(prod_done, 1)
                    waits(dve, "dve", (prod_done, 2 * g + u + 1), (agg_done, 2 * g + u - 1 if isinstance(g, int) else 2 * g))
                    V.tensor_reduce(out=msg[:, u, :], in_=prod[:, :].rearrange("p (n i) -> p n i", i=DB),
                                    axis=AX.X, op=ALU.add).then_inc(msg_ready, 1)

                def residual(g, a):
                    x_g = slot(g)[:, 2 * a:2 * a + 2, :].rearrange("p q d -> p (q d)")
                    waits(dve, "dve", (mm2_done, 2 * g + a + 1))
                    V.tensor_tensor(x_g, OUT[a][:, :], x_g, op=ALU.add).then_inc(res_ready, 1)

                def step(g, layer):
                    known = isinstance(g, int)
                    ahead = not known or g + 1 < GROUPS
                    if ahead or layer == 1:
                        root(g + 1)
                    if layer == 1:
                        waits(dve, "dve", (eT_done, g), (h_ready, g), (xe_gathered, 32 * g + 32))
                        normalise(hn_e[:, 0, :], xe[:, 0, :], Q)
                        normalise(hn_e[:, 1, :], xe[:, 1, :], Q + 1).then_inc(edge_rows_ready, 1)
                    else:
                        waits(dve, "dve", (eT_done, PAIRS), (h_ready, g), (psrc_loaded, 16 * (g - PAIRS + 1)),
                              (sum1_gathered, 32 * (g - PAIRS + 1)))
                        V.tensor_tensor(hn_e[:, :, :], psrc_in[:, :, :], sum1_in[:, :, :], op=ALU.add).then_inc(edge_rows_ready, 1)
                    waits(dve, "dve", (agg_done, 2 * g), (masks_ready, g))
                    V.tensor_copy(icols[:, :], inv_col[:, bass.ds(2 * g, 2)])
                    V.tensor_copy(dcols[:, :], dst_col[:, bass.ds(2 * g, 3)]).then_inc(cols_read, 1)
                    waits(dve, "dve", (cols_read, g + 1), (rows_loaded, 16 * (g + 1)))
                    for u in range(2):
                        V.tensor_scalar(onehot[:, u, :], rows[:, u, 1, :], relation_of_part[:, :], None, ALU.is_equal)
                        V.tensor_scalar(carried[:, u, :], rows[:, u, 0, :], dcols[:, u:u + 1], last_part[:, :], ALU.is_equal, ALU.mult)
                        last = V.scalar_tensor_tensor(out=same_dst[:, u, :], in0=rows[:, u, 0, :], scalar=dcols[:, u + 1:u + 2],
                                                      in1=upper[:, :], op0=ALU.is_equal, op1=ALU.mult)
                    last.then_inc(masks_ready, 1)
                    if ahead:
                        normalise_nodes(g + 1)
                    product(g, 0, layer)
                    residual(g, 0)
                    product(g, 1, layer)
                    residual(g, 1)
                    if layer == 1:
                        waits(dve, "dve", (eP_done, g + 1), (psrc_stored, 16 * g))
                        V.tensor_tensor(psrc_out[:, :, :], P1[1][:, :].rearrange("p (u d) -> p u d", u=2),
                                        bias1_row[:, :].unsqueeze(1).broadcast_to([P, 2, D]), op=ALU.add).then_inc(psrc_ready, 1)
                    if not known or g + 2 < GROUPS:
                        stats(g + 2, layer == 1)

                stats(0, False)
                root(0)
                normalise_nodes(0)
                stats(1, True)
                both_loops(dve, step)

            @block.scalar
            def _(act):
                A = nc.scalar.activation

                def roots(n):
                    waits(act, "act", (stats_ready, n + 1), (rstd_ready, n))
                    A(std[:, :], mv[:, :, 1], ACT.Sqrt, bias=eps_col[:, :]).then_inc(std_ready, 1)

                def save_hT(n):
                    waits(act, "act", (xT_done, n + 1), (mm1_done, 2 * n))
                    for a in range(2):
                        last = A(hT[:, :, 2 * a:2 * a + 2, :].rearrange("f k q p -> f q k p"),
                                 XT[a][:, :].rearrange("f (q k p) -> f q k p", q=2, k=K), ACT.Relu)
                    last.then_inc(hT_ready, 1)

                def save_o1(g, m):
                    waits(act, "act", (mm1_done, 2 * g + m + 1), (mm2_done, 2 * g))
                    A(o1T[:, m, :, :].rearrange("f q p -> f (q p)"), P1[m][:, :], ACT.Relu,
                      bias=bias1_col[:, m:m + 1]).then_inc(o1_ready, 1)

                def save_sums(g, u):
                    waits(act, "act", (agg_done, 2 * g + u + 1), (sums_stored, 16 * g))
                    A(sums[:, u, :], WX[0][:, 0:D], ACT.Copy).then_inc(sums_ready, 1)

                def step(g, layer):
                    known = isinstance(g, int)
                    waits(act, "act", (edge_rows_ready, g + 1), (cols_read, g + 1), (prod_done, 2 * g))
                    for u in range(2):
                        last = A(h_scaled[:, u, :], hn_e[:, u, :], ACT.Relu, scale=icols[:, u:u + 1])
                    last.then_inc(h_ready, 1)
                    save_o1(g, 0)
                    save_o1(g, 1)
                    if not known or g + 1 < GROUPS:
                        save_hT(g + 1)
                    save_sums(g, 0)
                    if layer == 1:
                        waits(act, "act", (eT_done, g + 1), (eP_done, g))
                        A(hTe[:, :, :, :].rearrange("f u k p -> f (u k p)"), P1[0][:, :], ACT.Relu).then_inc(hTe_ready, 1)
                    save_sums(g, 1)
                    if not known or g + 2 < GROUPS:
                        roots(g + 2)

                roots(0)
                save_hT(0)
                roots(1)
                both_loops(act, step)

            @block.tensor
            def _(pe):
                mm, T = nc.tensor.matmul, nc.tensor.transpose

                def turn_nodes(n):
                    waits(pe, "pe", (hn_ready, n + 1), (hT_ready, n))
                    for q in range(Q):
                        for k in range(K):
                            at = (q % 2) * D + k * P
                            last = T(XT[q // 2][:, at:at + P], hn[:, q, k * P:(k + 1) * P], ident[:, :])
                    last.then_inc(xT_done, 1)

                def layer_one(g, m):
                    for k in range(K):
                        last = mm(P1[m][:, :], root1_sb[:, k, m * P:(m + 1) * P],
                                  hT[:, k, :, :].rearrange("f q p -> f (q p)"), start=(k == 0), stop=(k == K - 1))
                    last.then_inc(mm1_done, 1)

                def layer_two(g, a):
                    for q in (2 * a, 2 * a + 1):
                        o = OUT[a][:, (q % 2) * D:(q % 2 + 1) * D]
                        mm(o, ones[:, :], bias2_parts[:, :], start=True, stop=False)
                        for k in range(K):
                            last = mm(o, o1T[:, k, q, :], root2_sb[:, k, :], start=False, stop=(k == K - 1))
                    last.then_inc(mm2_done, 1)

                def expand(g, u, layer):
                    for half in range(2):
                        last = mm(WX[half][:, :], onehot[:, u, :], w_parts[layer - 1][:, half * 512:half * 512 + 512],
                                  start=True, stop=True)
                    last.then_inc(wexp_done, 1)

                def aggregate(g, u):
                    waits(pe, "pe", (msg_ready, 2 * g + u + 1), (sums_ready, 2 * g + u))
                    mm(WX[0][:, 0:D], same_dst[:, u, :], msg[:, u, :], start=True, stop=False)
                    mm(WX[0][:, 0:D], carried[:, u, :], sums[:, 1 - u, :], start=False, stop=True).then_inc(agg_done, 1)

                def step(g, layer):
                    known = isinstance(g, int)
                    waits(pe, "pe", (hT_ready, g + 1), (o1_ready, 2 * g),
                          (hTe_ready, g if layer == 1 else PAIRS))
                    layer_one(g, 0)
                    waits(pe, "pe", (masks_ready, g + 1), (sums_ready, 2 * g))
                    expand(g, 0, layer)
                    waits(pe, "pe", (psrc_ready, g if layer == 1 else PAIRS))
                    layer_one(g, 1)
                    if not known or g + 1 < GROUPS:
                        turn_nodes(g + 1)
                    waits(pe, "pe", (o1_ready, 2 * g + 2), (res_ready, 2 * g))
                    layer_two(g, 0)
                    aggregate(g, 0)
                    if layer == 1:
                        for u in range(2):
                            for k in range(K):
                                last = T(P1[0][:, (u * K + k) * P:(u * K + k + 1) * P], hn_e[:, u, k * P:(k + 1) * P], ident[:, :])
                        last.then_inc(eT_done, 1)
                    waits(pe, "pe", (sums_ready, 2 * g + 1))
                    expand(g, 1, layer)
                    layer_two(g, 1)
                    if layer == 1:
                        waits(pe, "pe", (hTe_ready, g + 1))
                        for u in range(2):
                            for k in range(K):
                                last = mm(P1[1][:, u * D:(u + 1) * D], hTe[:, u, k, :], root1_sb[:, k, :],
                                          start=(k == 0), stop=(k == K - 1))
                        last.then_inc(eP_done, 1)
                    aggregate(g, 1)

                turn_nodes(0)
                both_loops(pe, step)

        xd_gathered = [sem(f"xd_gathered{h}") for h in range(2)]
        s_loaded = [sem(f"s_loaded{h}") for h in range(2)]
        fin_scattered = [sem(f"fin_scattered{h}") for h in range(2)]
        idxd_ready, idxf_ready = sem("idxd_ready"), sem("idxf_ready")
        bn3, stats3, std3, rstd3 = sem("bn3"), sem("stats3"), sem("std3"), sem("rstd3")
        hn3, resid3, xT3, hT3 = sem("hn3"), sem("resid3"), sem("xT3"), sem("hT3")
        mm3, o3, mm4, fin3 = sem("mm3"), sem("o3"), sem("mm4"), sem("fin3")
        H2 = PAIRS // 2
        assert PAIRS % 2 == 0

        with nc.Block() as block:
            @block.sync
            def _(sp):
                def load(j, h, i):
                    sp.dma_start(s1d[:, h, :, :], pair_rows(sum1, j)).then_inc(s_loaded[h], 16)
                    sp.dma_start(s2d[:, h, :, :], pair_rows(sum2, j)).then_inc(s_loaded[h], 16)

                load(0, 0, 0)
                load(1, 1, 0)

                def step(i, last):
                    for h in range(2):
                        j = 2 * i + h
                        if not last:
                            waits(sp, "sp", (mm3, j + 1), (resid3, j + 1))
                            load(j + 2, h, i + 1)

                with sp.Fori(0, H2 - 1) as i:
                    step(i, False)

            @block.gpsimd
            def _(pool):
                def gather(i, h):
                    j = 2 * i + h
                    waits(pool, "pool", (xd_gathered[1 - h], 32 * (i + h)), (hn3, j - 1 if isinstance(i, int) else j - 1),
                          (resid3, j - 1))
                    nc.gpsimd.tensor_copy(idx_xd[:, :], dsti_col[:, bass.ds(2 * j, 2)]).then_inc(idxd_ready, 1)
                    waits(pool, "pool", (idxd_ready, j + 1))
                    for u in range(2):
                        pool.indirect_dma_start(out=xd[:, h, u, :], out_offset=None, in_=x,
                                                in_offset=bass.IndirectOffsetOnAxis(ap=idx_xd[:, u:u + 1], axis=0),
                                                bounds_check=N - 1, oob_is_err=False).then_inc(xd_gathered[h], 16)

                def scatter(i, h):
                    j = 2 * i + h
                    waits(pool, "pool", (fin_scattered[1 - h], 32 * (i + h)), (fin3, j + 1))
                    nc.gpsimd.tensor_copy(idx_fin[:, :], out_col[:, bass.ds(2 * j, 2)]).then_inc(idxf_ready, 1)
                    waits(pool, "pool", (idxf_ready, j + 1))
                    for u in range(2):
                        pool.indirect_dma_start(out=out, out_offset=bass.IndirectOffsetOnAxis(ap=idx_fin[:, u:u + 1], axis=0),
                                                in_=final[:, h, u, :], in_offset=None,
                                                bounds_check=N - 1, oob_is_err=False).then_inc(fin_scattered[h], 16)

                gather(0, 0)
                gather(0, 1)
                with pool.Fori(0, H2 - 1) as i:
                    for h in range(2):
                        gather(i + 1, h)
                        scatter(i, h)
                for h in range(2):
                    scatter(H2 - 1, h)
                for h in range(2):
                    waits(pool, "pool", (fin_scattered[h], 32 * H2))

            def three(eng, step):
                with eng.Fori(0, H2 - 1) as i:
                    for h in range(2):
                        step(i, h, False, False)
                for h in range(2):
                    step(H2 - 1, h, True, h == 1)

            @block.vector
            def _(dve):
                V = nc.vector

                def stats(j, h, n):
                    waits(dve, "dve", (xd_gathered[h], 32 * n), (hn3, j), (std3, j))
                    for u in range(2):
                        last = V.bn_stats(bn[:, u, :], xd[:, h, u, :])
                    last.then_inc(bn3, 1)
                    waits(dve, "dve", (bn3, j + 1))
                    for u in range(2):
                        last = V.bn_aggr(mv[:, u, :], bn[:, u, :])
                    last.then_inc(stats3, 1)

                def prepare(j, h, n):
                    waits(dve, "dve", (std3, j + 1))
                    V.reciprocal(rstd[:, 0:2], std[:, 0:2]).then_inc(rstd3, 1)
                    waits(dve, "dve", (rstd3, j + 1), (xT3, j))
                    for u in range(2):
                        last = V.tensor_scalar(hn[:, u, :], xd[:, h, u, :], mv[:, u, 0:1], rstd[:, u:u + 1], ALU.subtract, ALU.mult)
                    last.then_inc(hn3, 1)
                    waits(dve, "dve", (s_loaded[h], 32 * n))
                    V.tensor_tensor(resid[:, h, :, :], xd[:, h, :, :], s2d[:, h, :, :], op=ALU.add).then_inc(resid3, 1)

                def step(i, h, last_i, last):
                    j = 2 * i + h
                    if not last:
                        prepare(j + 1, 1 - h, i + 1 + h)
                    waits(dve, "dve", (mm4, j + 1), (fin_scattered[h], 32 * i))
                    V.tensor_tensor(final[:, h, :, :].rearrange("p u d -> p (u d)"), OUT[0][:, :],
                                    resid[:, h, :, :].rearrange("p u d -> p (u d)"), op=ALU.add).then_inc(fin3, 1)
                    if not last_i:
                        stats(j + 2, h, i + 2)

                stats(0, 0, 1)
                prepare(0, 0, 1)
                stats(1, 1, 1)
                three(dve, step)

            @block.scalar
            def _(act):
                A = nc.scalar.activation

                def roots(j):
                    waits(act, "act", (stats3, j + 1), (rstd3, j))
                    A(std[:, 0:2], mv[:, 0:2, 1], ACT.Sqrt, bias=eps_col[:, :]).then_inc(std3, 1)

                def save_hT(j):
                    waits(act, "act", (xT3, j + 1), (mm3, j))
                    A(hT[:, :, 0:2, :].rearrange("f k u p -> f u k p"),
                      XT[0][:, :].rearrange("f (u k p) -> f u k p", u=2, k=K), ACT.Relu).then_inc(hT3, 1)

                def step(i, h, last_i, last):
                    j = 2 * i + h
                    waits(act, "act", (mm3, j + 1), (mm4, j))
                    for m in range(K):
                        done = A(o1T[:, m, 0:2, :].rearrange("f q p -> f (q p)"), P1[m][:, 0:2 * P], ACT.Relu,
                                 bias=bias1_col[:, m:m + 1])
                    done.then_inc(o3, 1)
                    if not last:
                        save_hT(j + 1)
                    if not last_i:
                        roots(j + 2)

                roots(0)
                save_hT(0)
                roots(1)
                three(act, step)

            @block.tensor
            def _(pe):
                mm, T = nc.tensor.matmul, nc.tensor.transpose

                def turn_rows(j):
                    waits(pe, "pe", (hn3, j + 1), (hT3, j))
                    for u in range(2):
                        for k in range(K):
                            last = T(XT[0][:, u * D + k * P:u * D + (k + 1) * P], hn[:, u, k * P:(k + 1) * P], ident[:, :])
                    last.then_inc(xT3, 1)

                def step(i, h, last_i, last):
                    j = 2 * i + h
                    waits(pe, "pe", (hT3, j + 1), (s_loaded[h], 32 * (i + 1)), (o3, j))
                    for m in range(K):
                        for k in range(K):
                            mm(P1[m][:, 0:2 * P], root1_sb[:, k, m * P:(m + 1) * P],
                               hT[:, k, 0:2, :].rearrange("f q p -> f (q p)"), start=(k == 0), stop=False)
                        for u in range(2):
                            done = mm(P1[m][:, u * P:(u + 1) * P], s1d[:, h, u, m * P:(m + 1) * P], ident[:, :],
                                      start=False, stop=(u == 1))
                    done.then_inc(mm3, 1)
                    if not last:
                        turn_rows(j + 1)
                    waits(pe, "pe", (o3, j + 1), (fin3, j))
                    for u in range(2):
                        o = OUT[0][:, u * D:(u + 1) * D]
                        mm(o, ones[:, :], bias2_parts[:, :], start=True, stop=False)
                        for k in range(K):
                            done = mm(o, o1T[:, k, u, :], root2_sb[:, k, :], start=False, stop=(k == K - 1))
                    done.then_inc(mm4, 1)

                turn_rows(0)
                three(pe, step)


_INS = ["x", "src", "dst", "edge_type_16", "L0_gnn_W1", "L0_gnn_root1", "L0_gnn_bias1",
        "L0_gnn_W2", "L0_gnn_root2", "L0_gnn_bias2"]


def kernel(**inputs):
    import numpy as _np
    import concourse.bacc as _bacc
    from concourse import mybir as _mybir
    from concourse.bass_utils import run_bass_kernel_spmd as _run

    nc = _bacc.Bacc("TRN2", target_bir_lowering=False, num_devices=1)
    arrays, args = {}, []
    for name in _INS:
        a = _np.ascontiguousarray(inputs[name])
        arrays[f"in_{name}"] = a
        args.append(nc.dram_tensor(f"in_{name}", a.shape, _mybir.dt.from_np(a.dtype), kind="ExternalInput").ap())
    shape = tuple(inputs["x"].shape)
    args.append(nc.dram_tensor("out_0", shape, _mybir.dt.float32, kind="ExternalOutput").ap())
    build(nc, *args)
    r = _run(nc, [arrays], core_ids=[0])
    return r.results[0]["out_0"]
```

```python
import concourse.bass as bass
import numpy as np
from concourse import mybir
from contextlib import ExitStack

F32, BF16, I32 = mybir.dt.float32, mybir.dt.bfloat16, mybir.dt.int32
ACT, ALU, AX = mybir.ActivationFunctionType, mybir.AluOpType, mybir.AxisListType
P = 128
EPS = 1e-5


def build(nc, x, src, dst, edge_type, w1, root1, bias1, w2, root2, bias2, out):
    N, D = x.shape
    E = src.shape[0]
    R, B, DB, _ = w1.shape
    K = D // P
    Q = 4
    GROUP = Q * P
    COLS = -(-E // P)
    COLS += COLS % 2
    EP = COLS * P
    PAIRS = COLS // 2
    GROUPS = -(-N // GROUP)
    assert GROUPS == 2 * PAIRS and K == 2 and B * DB == D
    LAST_ROW = N - GROUP
    NO_NODE = 1 << 17
    NOT_LAST = 1 << 20
    assert N <= NO_NODE and NO_NODE + NOT_LAST < 1 << 24
    ZERO_ROW = EP
    TABLE = -(-N // P) * P
    W = B * DB * DB

    ctx = ExitStack()
    with ctx:
        def sb(name, shape, dt=F32):
            return ctx.enter_context(nc.sbuf_tensor(name, shape, dt))

        def sem(name):
            return ctx.enter_context(nc.semaphore(name))

        def scratch(name, shape, dt=F32):
            return nc.dram_tensor(name, shape, dt, kind="Internal").ap()

        dst_shifted = scratch("dst_shifted", [EP + 2])
        edge_kinds = scratch("edge_kinds", [5, EP])
        edge_rows = scratch("edge_rows", [2 * COLS, 2, P])
        last_edge_of = scratch("last_edge_of", [TABLE, 1], I32)
        p_src = scratch("p_src", [EP, D])
        sum1 = scratch("sum1", [EP + 1, D])
        sum2 = scratch("sum2", [EP, D])

        ident = sb("ident", [P, P])
        upper = sb("upper", [P, P])
        last_part = sb("last_part", [P, 1])
        ones = sb("ones", [P, P], BF16)
        relation_of_part = sb("relation_of_part", [P, 1])
        eps_col = sb("eps_col", [P, 1])
        root1_sb = sb("root1_sb", [P, K, D])
        root2_sb = sb("root2_sb", [P, K, D])
        bias1_col = sb("bias1_col", [P, K])
        bias1_parts = sb("bias1_parts", [P, D], BF16)
        bias2_parts = sb("bias2_parts", [P, D], BF16)
        w_parts = [sb(f"w{n}_parts", [P, W], BF16) for n in (1, 2)]
        dst_col = sb("dst_col", [P, 1 + 2 * COLS + 2])
        inv_col = sb("inv_col", [P, 2 * COLS + 2])
        src_col = sb("src_col", [P, 2 * COLS + 2], I32)
        out_col = sb("out_col", [P, COLS], I32)
        edge_col = sb("edge_col", [P, COLS], I32)
        dsti_col = sb("dsti_col", [P, COLS + 4], I32)
        x_sb = sb("x_sb", [P, 4, Q, D])
        nbn, ebn = sb("nbn", [P, Q, 6]), sb("ebn", [P, 2, 6])
        nmv, emv = sb("nmv", [P, Q, 2]), sb("emv", [P, 2, 2])
        nstd, estd = sb("nstd", [P, Q]), sb("estd", [P, 2])
        nrstd, erstd = sb("nrstd", [P, Q]), sb("erstd", [P, 2])
        nnmr, enmr = sb("nnmr", [P, Q]), sb("enmr", [P, 2])
        hn = sb("hn", [P, Q, D])
        hT = sb("hT", [P, K, Q, P])
        o1T = sb("o1T", [P, K, Q, P])
        xe = sb("xe", [P, 2, D])
        he = sb("he", [P, 2, D])
        hTe = sb("hTe", [P, 2, K, P])
        psrc_out = sb("psrc_out", [P, 2, D])
        psrc_in = sb("psrc_in", [P, 2, D])
        sum1_in = sb("sum1_in", [P, 2, D])
        h_scaled = sb("h_scaled", [P, 2, D])
        rows = sb("rows", [P, 2, 2, P])
        dcols = sb("dcols", [P, 3])
        icols = sb("icols", [P, 2])
        same_dst = sb("same_dst", [P, 2, P])
        carried = sb("carried", [P, 2, P])
        onehot = sb("onehot", [P, 2, P], BF16)
        prod = sb("prod", [P, W])
        msg = sb("msg", [P, 2, D])
        sums = sb("sums", [P, 2, D])
        idx_src = sb("idx_src", [P, 2], I32)
        idx_out = sb("idx_out", [P, 2], I32)
        idx_edge = sb("idx_edge", [P, 2], I32)
        idx_sum = sb("idx_sum", [P, 2], I32)
        xd = sb("xd", [P, 2, 2, D])
        s1d = sb("s1d", [P, 2, 2, D])
        s2d = sb("s2d", [P, 2, 2, D])
        resid = sb("resid", [P, 2, 2, D])
        final = sb("final", [P, 2, 2, D])
        idx_xd = sb("idx_xd", [P, 2, 2], I32)
        idx_fin = sb("idx_fin", [P, 2, 2], I32)

        bank = [ctx.enter_context(nc.psum_tensor(f"bank{i}", [P, 512], F32)) for i in range(8)]
        XT, P1, OUT, WX = bank[0:2], bank[2:4], bank[4:6], bank[6:8]

        turn = {e: sem(f"turn_{e}") for e in ("sp", "pool", "dve", "act", "pe")}

        def waits(eng, name, *pairs):
            some = False
            for s, n in pairs:
                if not (isinstance(n, int) and n <= 0):
                    eng.wait_ge(s, n)
                    some = True
            if some:
                eng.sem_inc(turn[name], 1)

        NB = EP // P
        FULL = E // NB
        REST = E - FULL * NB
        with ExitStack() as setup:
            def tb(name, shape, dt=F32):
                return setup.enter_context(nc.sbuf_tensor(name, shape, dt))

            raw = tb("raw", [P, 3, NB], I32)
            kinds = tb("kinds", [P, 5, NB])
            near = tb("near", [P, 2, NB])
            same = tb("same", [P, 2, NB])
            local = tb("local", [P, R, NB])
            onehot_s = tb("onehot_s", [P, R, NB])
            same_rep = tb("same_rep", [P, R, NB])
            run = tb("run", [P, NB])
            count = tb("count", [P, R, NB])
            relation_i = tb("relation_i", [P, R], I32)
            relation_f = tb("relation_f", [P, R])
            end_run = tb("end_run", [P, 2, R])
            carry_t = tb("carry_t", [R, 3, P])
            carry = tb("carry", [P, R])
            minus = tb("minus", [1, 2])
            table0 = tb("table0", [P, TABLE // P], I32)
            zero_row = tb("zero_row", [1, D])
            kind_rows = tb("kind_rows", [P, 2, 5, P])
            part_i = tb("part_i", [P, 1], I32)
            w_f = [tb(f"w{n}_f", [P, W]) for n in (1, 2)]
            w_r = tb("w_r", [P, W])
            b_f = [tb(f"b{n}_f", [P, D]) for n in (1, 2)]
            w_low = tb("w_low", [P, 2, W], BF16)
            back = tb("back", [P, 1])
            flag_row = tb("flag_row", [1, 1])
            flag = tb("flag", [1, 1], I32)
            place = tb("place", [P, R * NB], I32)
            edge_i = tb("edge_i", [P, NB], I32)
            edge_f = tb("edge_f", [P, NB])
            rank = tb("rank", [P, NB])
            rank_i = tb("rank_i", [P, NB], I32)
            of_edge = tb("of_edge", [P, 4])
            rank_col = tb("rank_col", [P, 1], I32)
            payload = tb("payload", [P, 4], I32)
            sorted_in = tb("sorted_in", [P, NB, 4], I32)
            sorted_edges = scratch("sorted_edges", [EP, 4], I32)

            padded = sem("padded")
            edges_in = sem("edges_in")
            consts_in = sem("consts_in")
            pool_consts = sem("pool_consts")
            dst_out = sem("dst_out")
            near_in = sem("near_in")
            kinds_ready = sem("kinds_ready")
            kinds_out = sem("kinds_out")
            kind_rows_in = sem("kind_rows_in")
            rows_out = sem("rows_out")
            table_out = sem("table_out")
            v = sem("setup_dve_step")
            t_done = sem("setup_transposed")
            cols_ready = sem("cols_ready")
            back_ready, back_turned, flag_ready = sem("back_ready"), sem("back_turned"), sem("flag_ready")
            chunk_in, chunk_used = sem("chunk_in"), sem("chunk_used")
            cols_taken, compared, counted, ranked = sem("cols_taken"), sem("compared"), sem("counted"), sem("ranked")
            rank_ready, staged, moved = sem("rank_ready"), sem("staged"), sem("moved")
            all_moved, sorted_ready, unpacked = sem("all_moved"), sem("sorted_ready"), sem("unpacked")
            dst_out2, near_in2 = sem("dst_out2"), sem("near_in2")
            CHUNK = R * NB
            CHUNKS = EP // CHUNK
            assert CHUNKS * CHUNK == EP

            with nc.Block() as block:
                @block.sync
                def _(sp):
                    sp.wait_ge(padded, 1)
                    for k, a in enumerate((dst, edge_type, src)):
                        sp.dma_start(raw[0:FULL, k, :], a[0:FULL * NB].rearrange("(p c) -> p c", c=NB)).then_inc(edges_in, 16)
                        sp.dma_start(raw[FULL:FULL + 1, k, 0:REST], a[FULL * NB:E].rearrange("(p c) -> p c", p=1)).then_inc(edges_in, 16)
                    sp.wait_ge(padded, 2)
                    for n, w in enumerate((w1, w2)):
                        for q in range(3):
                            sp.dma_start(w_f[n][32 * q:32 * q + R, :], w.rearrange("r b i o -> r (b i o)")).then_inc(consts_in, 16)
                    for q in range(3):
                        for n, b in enumerate((bias1, bias2)):
                            sp.dma_start(b_f[n][32 * q:32 * q + 1, :], b.rearrange("(a d) -> a d", a=1)).then_inc(consts_in, 16)
                    sp.dma_start(root1_sb[:, :, :], root1.rearrange("(k p) d -> p k d", p=P)).then_inc(consts_in, 16)
                    sp.dma_start(root2_sb[:, :, :], root2.rearrange("(k p) d -> p k d", p=P)).then_inc(consts_in, 16)
                    with nc.allow_non_contiguous_dma(reason="one column per feature chunk"):
                        sp.dma_start(bias1_col[:, :], bias1.rearrange("(k p) -> p k", p=P)).then_inc(consts_in, 16)
                    sp.wait_ge(kinds_ready, 1)
                    sp.dma_start(dst_shifted[1:EP + 1].rearrange("(p c) -> p c", c=NB), kinds[:, 0, :]).then_inc(dst_out, 16)
                    sp.dma_start(dst_shifted[0:1].rearrange("(p c) -> p c", p=1), minus[:, 0:1]).then_inc(dst_out, 16)
                    sp.dma_start(dst_shifted[EP + 1:EP + 2].rearrange("(p c) -> p c", p=1), minus[:, 1:2]).then_inc(dst_out, 16)
                    sp.wait_ge(dst_out, 48)
                    for k in range(2):
                        sp.dma_start(near[:, k, :], dst_shifted[2 * k:2 * k + EP].rearrange("(p c) -> p c", c=NB)).then_inc(near_in, 16)
                    sp.wait_ge(flag_ready, 1)
                    unsorted = sp.value_load(flag[0:1, 0:1], min_val=0, max_val=1)
                    with sp.If(unsorted > 0):
                        for n in range(CHUNKS):
                            sp.wait_ge(chunk_used, n)
                            sp.dma_start(local[:, :, :].rearrange("p r c -> p (r c)"),
                                         dst_shifted[1 + n * CHUNK:1 + (n + 1) * CHUNK].partition_broadcast(P)).then_inc(chunk_in, 16)
                        sp.wait_ge(all_moved, 1)
                        sp.dma_start(sorted_in[:, :, :], sorted_edges.rearrange("(p c) k -> p c k", c=NB)).then_inc(sorted_ready, 16)
                        sp.wait_ge(unpacked, 1)
                        sp.dma_start(dst_shifted[1:EP + 1].rearrange("(p c) -> p c", c=NB), kinds[:, 0, :]).then_inc(dst_out2, 16)
                        sp.wait_ge(dst_out2, 16)
                        for k in range(2):
                            sp.dma_start(near[:, k, :], dst_shifted[2 * k:2 * k + EP].rearrange("(p c) -> p c", c=NB)).then_inc(near_in2, 16)
                    sp.wait_ge(kinds_ready, 2)
                    sp.dma_start(edge_kinds.rearrange("k (p c) -> p k c", c=NB), kinds[:, :, :]).then_inc(kinds_out, 16)
                    sp.wait_ge(kinds_out, 16)
                    by_tile = edge_kinds.rearrange("k (c p) -> c k p", p=P)
                    sp.dma_start(kind_rows[:, 0, :, :], by_tile[0:P]).then_inc(kind_rows_in, 16)
                    sp.dma_start(kind_rows[0:COLS - P, 1, :, :], by_tile[P:COLS]).then_inc(kind_rows_in, 16)
                    sp.wait_ge(kind_rows_in, 32)
                    for again in (0, COLS):
                        sp.dma_start(edge_rows[again:again + P], kind_rows[:, 0, 0:2, :]).then_inc(rows_out, 16)
                        sp.dma_start(edge_rows[again + P:again + COLS], kind_rows[0:COLS - P, 1, 0:2, :]).then_inc(rows_out, 16)
                    sp.wait_ge(pool_consts, 1)
                    sp.dma_start(last_edge_of.rearrange("(p c) a -> p (c a)", p=P), table0[:, :]).then_inc(table_out, 16)
                    sp.dma_start(sum1[ZERO_ROW:ZERO_ROW + 1, :], zero_row[:, :]).then_inc(table_out, 16)
                    sp.wait_ge(rows_out, 64)
                    sp.wait_ge(table_out, 32)
                    sp.wait_ge(consts_in, 15 * 16)

                @block.gpsimd
                def _(pool):
                    pool.memset(ident[:, :], 0.0).then_inc(turn["pool"], 1)
                    pool.memset(upper[:, :], 1.0).then_inc(turn["pool"], 1)
                    pool.memset(table0[:, :], ZERO_ROW)
                    pool.memset(zero_row[:, :], 0.0)
                    pool.iota(relation_i[:, :], pattern=[[1, R]], base=0, channel_multiplier=0)
                    pool.iota(edge_col[:, :], pattern=[[P, COLS]], base=0, channel_multiplier=1)
                    pool.iota(part_i[:, :], pattern=[[0, 1]], base=0, channel_multiplier=1)
                    pool.iota(place[:, :], pattern=[[1, R * NB]], base=0, channel_multiplier=0)
                    pool.iota(edge_i[:, :], pattern=[[1, NB]], base=0, channel_multiplier=NB)
                    pool.memset(payload[:, :], 0)
                    pool.wait_ge(turn["pool"], 2)
                    pool.affine_select(out=ident[:, :], in_=ident[:, :], compare_op=ALU.not_equal, fill=1.0,
                                       base=0, pattern=[[-1, P]], channel_multiplier=1)
                    pool.affine_select(out=upper[:, :], in_=upper[:, :], compare_op=ALU.is_ge, fill=0.0,
                                       base=0, pattern=[[1, P]], channel_multiplier=-1).then_inc(pool_consts, 1)
                    pool.wait_ge(flag_ready, 1)
                    unsorted = pool.value_load(flag[0:1, 0:1], min_val=0, max_val=1)
                    with pool.If(unsorted > 0):
                        pool.wait_ge(rank_ready, 1)
                        with pool.Fori(0, NB) as c:
                            waits(pool, "pool", (moved, 16 * c))
                            nc.gpsimd.tensor_copy(rank_col[:, :], rank_i[:, bass.ds(c, 1)])
                            nc.gpsimd.tensor_copy(payload[:, 0:3].unsqueeze(2), raw[:, :, bass.ds(c, 1)]).then_inc(staged, 1)
                            waits(pool, "pool", (staged, c + 1))
                            pool.indirect_dma_start(out=sorted_edges, out_offset=bass.IndirectOffsetOnAxis(ap=rank_col[:, :], axis=0),
                                                    in_=payload[:, :], in_offset=None).then_inc(moved, 16)
                        waits(pool, "pool", (moved, 16 * NB))
                        pool.sem_inc(all_moved, 1)

                @block.vector
                def _(dve):
                    step = [0]

                    def do(ins):
                        step[0] += 1
                        ins.then_inc(v, 1)

                    def settle():
                        dve.wait_ge(v, step[0])

                    V = nc.vector
                    do(V.memset(raw[:, 0, :], NO_NODE))
                    settle()
                    V.memset(raw[:, 1:3, :], 0).then_inc(padded, 1)
                    for t in (*w_f, *b_f):
                        do(V.memset(t[:, :], 0.0))
                    do(V.memset(minus[:, :], -1.0))
                    do(V.memset(eps_col[:, :], EPS))
                    do(V.memset(ones[:, :], 1.0))
                    do(V.memset(sums[:, :, :], 0.0))
                    do(V.memset(xd[:, :, :, :], 0.0))
                    do(V.memset(dst_col[:, :], -1.0))
                    do(V.memset(inv_col[:, :], 1.0))
                    do(V.memset(src_col[:, :], 0))
                    do(V.memset(dsti_col[:, :], 0))
                    settle()
                    dve.sem_inc(padded, 1)
                    dve.wait_ge(edges_in, 96)
                    do(V.tensor_copy(kinds[:, 0:3, :], raw[:, :, :]))
                    settle()
                    dve.sem_inc(kinds_ready, 1)
                    dve.wait_ge(pool_consts, 1)
                    do(V.tensor_copy(relation_f[:, :], relation_i[:, :]))
                    for q in range(4):
                        do(V.tensor_scalar(relation_of_part[32 * q:32 * q + 32, :], part_i[32 * q:32 * q + 32, :],
                                           float(-32 * q), None, ALU.add))
                    do(V.tensor_copy(last_part[:, :], ident[:, P - 1:P]))
                    settle()
                    dve.wait_ge(near_in, 32)
                    do(V.tensor_tensor(same[:, 0, :], kinds[:, 0, :], near[:, 0, :], op=ALU.is_lt))
                    settle()
                    do(V.tensor_reduce(out=back[:, :], in_=same[:, 0, :], axis=AX.X, op=ALU.max))
                    settle()
                    dve.sem_inc(back_ready, 1)
                    dve.wait_ge(back_turned, 1)
                    do(V.tensor_reduce(out=flag_row[:, :], in_=bank[1][0:1, 0:P], axis=AX.X, op=ALU.max))
                    settle()
                    do(V.tensor_copy(flag[:, :], flag_row[:, :]))
                    do(V.tensor_copy(edge_f[:, :], edge_i[:, :]))
                    do(V.memset(rank[:, :], 0.0))
                    settle()
                    dve.sem_inc(flag_ready, 1)
                    unsorted = dve.value_load(flag[0:1, 0:1], min_val=0, max_val=1)
                    with dve.If(unsorted > 0):
                        for n in range(CHUNKS):
                            dve.wait_ge(chunk_in, 16 * (n + 1))
                            with dve.Fori(0, NB) as c:
                                t = c + n * NB
                                waits(dve, "dve", (counted, t), (ranked, t))
                                V.tensor_copy(of_edge[:, 0:1], kinds[:, 0, bass.ds(c, 1)])
                                V.tensor_scalar(of_edge[:, 1:2], edge_f[:, bass.ds(c, 1)], float(-n * CHUNK), None,
                                                ALU.add).then_inc(cols_taken, 1)
                                waits(dve, "dve", (cols_taken, t + 1))
                                low = onehot_s[:, :, :].rearrange("p r c -> p (r c)")
                                equal = same_rep[:, :, :].rearrange("p r c -> p (r c)")
                                before = count[:, :, :].rearrange("p r c -> p (r c)")
                                dsts = local[:, :, :].rearrange("p r c -> p (r c)")
                                V.tensor_scalar(low, dsts, of_edge[:, 0:1], None, ALU.is_lt)
                                V.tensor_scalar(equal, dsts, of_edge[:, 0:1], None, ALU.is_equal).then_inc(compared, 1)
                                waits(dve, "dve", (compared, 2 * t + 1))
                                V.scalar_tensor_tensor(out=before, in0=place[:, :], scalar=of_edge[:, 1:2], in1=equal,
                                                       op0=ALU.is_lt, op1=ALU.mult).then_inc(compared, 1)
                                waits(dve, "dve", (compared, 2 * t + 2))
                                V.tensor_reduce(out=of_edge[:, 2:3], in_=low, axis=AX.X, op=ALU.add)
                                V.tensor_reduce(out=of_edge[:, 3:4], in_=before, axis=AX.X, op=ALU.add).then_inc(counted, 1)
                                waits(dve, "dve", (counted, t + 1))
                                V.scalar_tensor_tensor(out=rank[:, bass.ds(c, 1)], in0=of_edge[:, 2:3], scalar=of_edge[:, 3:4],
                                                       in1=rank[:, bass.ds(c, 1)], op0=ALU.add, op1=ALU.add).then_inc(ranked, 1)
                            waits(dve, "dve", (ranked, NB * (n + 1)))
                            dve.sem_inc(chunk_used, 1)
                        V.tensor_copy(rank_i[:, :], rank[:, :]).then_inc(rank_ready, 1)
                        dve.wait_ge(sorted_ready, 16)
                        V.tensor_copy(kinds[:, 0:3, :], sorted_in[:, :, 0:3].rearrange("p c k -> p k c")).then_inc(unpacked, 1)
                        dve.wait_ge(near_in2, 32)
                    do(V.tensor_tensor(onehot_s[:, :, :], kinds[:, 1:2, :].broadcast_to([P, R, NB]),
                                       relation_f[:, :].unsqueeze(2).broadcast_to([P, R, NB]), op=ALU.is_equal))
                    for k in range(2):
                        do(V.tensor_tensor(same[:, k, :], kinds[:, 0, :], near[:, k, :], op=ALU.is_equal))
                    settle()
                    do(V.scalar_tensor_tensor(out=kinds[:, 4, :], in0=same[:, 1, :], scalar=float(NOT_LAST),
                                              in1=kinds[:, 0, :], op0=ALU.mult, op1=ALU.add))
                    for k in range(2):
                        def way(t):
                            return t if k == 0 else t[:, ::-1]
                        first = 0 if k == 0 else NB - 1
                        do(V.tensor_copy(same_rep[:, :, :], same[:, k:k + 1, :].broadcast_to([P, R, NB])))
                        settle()
                        do(V.memset(same_rep[:, :, first:first + 1], 0.0))
                        do(V.tensor_tensor_scan(way(run[:, :]), way(same[:, k, :]), way(same[:, k, :]), 1.0,
                                                op0=ALU.mult, op1=ALU.min))
                        settle()
                        do(V.tensor_tensor_scan(way(local[:, :, :].rearrange("p r c -> p (r c)")),
                                                way(same_rep[:, :, :].rearrange("p r c -> p (r c)")),
                                                way(onehot_s[:, :, :].rearrange("p r c -> p (r c)")), 0.0,
                                                op0=ALU.mult, op1=ALU.add))
                        settle()
                        end = NB - 1 - first
                        do(V.tensor_copy(end_run[:, 0, :], local[:, :, end]))
                        do(V.tensor_copy(end_run[:, 1, :], run[:, end:end + 1].broadcast_to([P, R])))
                        settle()
                        dve.sem_inc(cols_ready, 1)
                        dve.wait_ge(t_done, 1 + 2 * k)
                        do(V.tensor_copy(carry_t[:, 0:2, :], bank[0][0:R, 0:2 * P].rearrange("r (a p) -> r a p", a=2)))
                        settle()
                        do(V.memset(carry_t[:, 2, :], 0.0))
                        settle()
                        if k == 0:
                            do(V.tensor_tensor_scan(carry_t[:, 2, 1:P], carry_t[:, 1, 0:P - 1], carry_t[:, 0, 0:P - 1], 0.0,
                                                    op0=ALU.mult, op1=ALU.add))
                        else:
                            do(V.tensor_tensor_scan(carry_t[:, 2, 0:P - 1][:, ::-1], carry_t[:, 1, 1:P][:, ::-1],
                                                    carry_t[:, 0, 1:P][:, ::-1], 0.0, op0=ALU.mult, op1=ALU.add))
                        settle()
                        dve.sem_inc(cols_ready, 1)
                        dve.wait_ge(t_done, 2 + 2 * k)
                        do(V.tensor_copy(carry[:, :], bank[0][:, 256:256 + R]))
                        settle()
                        do(V.tensor_tensor(same_rep[:, :, :], run[:, :].unsqueeze(1).broadcast_to([P, R, NB]),
                                           carry[:, :].unsqueeze(2).broadcast_to([P, R, NB]), op=ALU.mult))
                        settle()
                        if k == 0:
                            do(V.tensor_tensor(count[:, :, :], local[:, :, :], same_rep[:, :, :], op=ALU.add))
                        else:
                            do(V.tensor_tensor(local[:, :, :], local[:, :, :], same_rep[:, :, :], op=ALU.add))
                            settle()
                            do(V.tensor_tensor(count[:, :, :], count[:, :, :], local[:, :, :], op=ALU.add))
                        settle()
                    do(V.tensor_tensor(count[:, :, :], count[:, :, :], onehot_s[:, :, :], op=ALU.mult))
                    settle()
                    do(V.tensor_reduce(out=run[:, :], in_=count[:, :, :].rearrange("p r c -> p c r"), axis=AX.X, op=ALU.add))
                    settle()
                    do(V.tensor_scalar(run[:, :], run[:, :], -1.0, 1.0, ALU.add, ALU.max))
                    settle()
                    do(V.reciprocal(kinds[:, 3, :], run[:, :]))
                    settle()
                    dve.sem_inc(kinds_ready, 1)
                    dve.wait_ge(consts_in, 15 * 16)
                    for dest, whole, n in ((w_parts[0], w_f[0], W), (w_parts[1], w_f[1], W), (bias1_parts, b_f[0], D),
                                           (bias2_parts, b_f[1], D)):
                        part = w_low[:, :, 0:n]
                        do(V.memset(dest[:, :], 0.0))
                        if n == W:
                            do(V.tensor_copy(w_r[:, 0:n].rearrange("p (b o i) -> p b o i", o=DB, i=DB),
                                             whole[:, :].rearrange("p (b i o) -> p b o i", o=DB, i=DB)))
                        else:
                            do(V.tensor_copy(w_r[:, 0:n], whole[:, :]))
                        settle()
                        do(V.tensor_copy(dest[:, :], w_r[:, 0:n]))
                        settle()
                        do(V.tensor_tensor(w_r[:, 0:n], w_r[:, 0:n], dest[:, :], op=ALU.subtract))
                        settle()
                        do(V.tensor_copy(part[:, 0, :], w_r[:, 0:n]))
                        settle()
                        do(V.tensor_tensor(w_r[:, 0:n], w_r[:, 0:n], part[:, 0, :], op=ALU.subtract))
                        do(V.tensor_copy(dest[32:64, :], part[32:64, 0, :]))
                        settle()
                        do(V.tensor_copy(dest[64:96, :], w_r[64:96, 0:n]))
                        do(V.memset(dest[96:128, :], 0.0))
                        settle()
                    dve.wait_ge(t_done, 5)
                    kind_at = lambda s: bank[2 + s // 2][:, (s % 2) * 256:(s % 2) * 256 + COLS]
                    for again in (0, COLS):
                        do(V.tensor_copy(dst_col[:, 1 + again:1 + again + COLS], kind_at(0)))
                        do(V.tensor_copy(src_col[:, again:again + COLS], kind_at(1)))
                        do(V.tensor_copy(inv_col[:, again:again + COLS], kind_at(2)))
                    do(V.tensor_copy(out_col[:, :], kind_at(3)))
                    do(V.tensor_copy(dsti_col[:, 0:COLS], kind_at(0)))
                    settle()

                @block.tensor
                def _(pe):
                    T = nc.tensor.transpose
                    pe.wait_ge(pool_consts, 1)
                    pe.wait_ge(back_ready, 1)
                    T(bank[1][0:1, 0:P], back[:, :], ident[:, :]).then_inc(back_turned, 1)
                    for k in range(2):
                        pe.wait_ge(cols_ready, 1 + 2 * k)
                        T(bank[0][0:R, 0:P], end_run[:, 0, :], ident[:, :])
                        T(bank[0][0:R, P:2 * P], end_run[:, 1, :], ident[:, :]).then_inc(t_done, 1)
                        pe.wait_ge(cols_ready, 2 + 2 * k)
                        T(bank[0][:, 256:256 + R], carry_t[:, 2, :], ident[0:R, 0:R]).then_inc(t_done, 1)
                    pe.wait_ge(kind_rows_in, 32)
                    for s, k in enumerate((0, 2, 3, 4)):
                        at = (s % 2) * 256
                        T(bank[2 + s // 2][:, at:at + P], kind_rows[:, 0, k, :], ident[:, :])
                        last = T(bank[2 + s // 2][:, at + P:at + COLS], kind_rows[0:COLS - P, 1, k, :],
                                 ident[0:COLS - P, 0:COLS - P])
                    last.then_inc(t_done, 1)

        x_loaded, x_stored = sem("x_loaded"), sem("x_stored")
        nbn_done, nstats_ready, nstd_ready, nroot_ready = sem("nbn_done"), sem("nstats_ready"), sem("nstd_ready"), sem("nroot_ready")
        ebn_done, estats_ready, estd_ready, eroot_ready = sem("ebn_done"), sem("estats_ready"), sem("estd_ready"), sem("eroot_ready")
        hn_ready, xT_done, hT_ready = sem("hn_ready"), sem("xT_done"), sem("hT_ready")
        mm1_done, o1_ready, mm2_done, res_ready = sem("mm1_done"), sem("o1_ready"), sem("mm2_done"), sem("res_ready")
        rows_loaded, cols_read, masks_ready = sem("rows_loaded"), sem("cols_read"), sem("masks_ready")
        xe_gathered, table_scattered, idx_ready = sem("xe_gathered"), sem("table_scattered"), sem("idx_ready")
        he_ready, hl1_ready, h_ready = sem("he_ready"), sem("hl1_ready"), sem("h_ready")
        eT_done, hTe_ready, eP_done, psrc_ready = sem("eT_done"), sem("hTe_ready"), sem("eP_done"), sem("psrc_ready")
        psrc_stored, psrc_loaded = sem("psrc_stored"), sem("psrc_loaded")
        wexp_done, prod_done, msg_ready = sem("wexp_done"), sem("prod_done"), sem("msg_ready")
        agg_done, sums_ready, sums_stored = sem("agg_done"), sem("sums_ready"), sem("sums_stored")
        table_read, idx2_ready, sum1_gathered = sem("table_read"), sem("idx2_ready"), sem("sum1_gathered")

        LOOKAHEAD = 3
        PEEL = GROUPS - LOOKAHEAD - 1

        def nodes_of(t, g):
            start = g * GROUP if not isinstance(g, int) else min(g * GROUP, LAST_ROW)
            return t[bass.ds(start, GROUP), :].rearrange("(p q) d -> p q d", q=Q)

        def slot(g):
            return x_sb[:, bass.ds(g % 4, 1), :, :].rearrange("p a q d -> p (a q) d")

        def pair_rows(t, pair):
            return t[bass.ds(pair * 2 * P, 2 * P), :].rearrange("(u p) d -> p u d", p=P)

        def both_loops(eng, step):
            with eng.Fori(0, PAIRS) as g:
                step(g, 1)
            with eng.Fori(PAIRS, PEEL) as g:
                step(g, 2)
            for g in range(PEEL, GROUPS):
                step(g, 2)

        with nc.Block() as block:
            @block.sync
            def _(sp):
                def load_x(g):
                    sp.dma_start(slot(g), nodes_of(x, g)).then_inc(x_loaded, 16)

                def load_rows(g):
                    sp.dma_start(rows[:, :, :, :].rearrange("p u k e -> p (u k e)"),
                                 edge_rows[bass.ds(2 * g, 2)].rearrange("u k e -> (u k e)").partition_broadcast(P)
                                 ).then_inc(rows_loaded, 16)

                def load_psrc(pair):
                    sp.dma_start(psrc_in[:, :, :], pair_rows(p_src, pair)).then_inc(psrc_loaded, 16)

                for g in range(LOOKAHEAD):
                    load_x(g)
                    waits(sp, "sp", (x_loaded, 16 * (g + 1)))
                load_rows(0)

                def step(g, layer):
                    known = isinstance(g, int)
                    if not known or g + LOOKAHEAD < GROUPS:
                        waits(sp, "sp", (x_stored, 16 * g), (x_loaded, 16 * (g + LOOKAHEAD)))
                        load_x(g + LOOKAHEAD)
                    if layer == 2 and (not known or g + 1 < GROUPS):
                        waits(sp, "sp", (hl1_ready, g - PAIRS + 1))
                        load_psrc(g + 1 - PAIRS)
                    if not known or g + 1 < GROUPS:
                        waits(sp, "sp", (masks_ready, g + 1))
                        load_rows(g + 1)
                    if known and g == GROUPS - 1:
                        waits(sp, "sp", (x_stored, 16 * g))
                    waits(sp, "sp", (res_ready, 2 * g + 2))
                    sp.dma_start(nodes_of(out, g), slot(g)).then_inc(x_stored, 16)
                    if layer == 1:
                        waits(sp, "sp", (psrc_ready, g + 1))
                        sp.dma_start(pair_rows(p_src, g), psrc_out[:, :, :]).then_inc(psrc_stored, 16)
                    waits(sp, "sp", (sums_ready, 2 * g + 2))
                    sp.dma_start(pair_rows(sum1 if layer == 1 else sum2, g if layer == 1 else g - PAIRS),
                                 sums[:, :, :]).then_inc(sums_stored, 16)

                with sp.Fori(0, PAIRS) as g:
                    step(g, 1)
                waits(sp, "sp", (psrc_stored, 16 * PAIRS))
                load_psrc(0)
                with sp.Fori(PAIRS, PEEL) as g:
                    step(g, 2)
                for g in range(PEEL, GROUPS):
                    step(g, 2)
                waits(sp, "sp", (x_stored, 16 * GROUPS), (sums_stored, 16 * GROUPS))

            @block.gpsimd
            def _(pool):
                def at(ap):
                    return bass.IndirectOffsetOnAxis(ap=ap, axis=0)

                def source_indices(g):
                    waits(pool, "pool", (xe_gathered, 32 * g))
                    nc.gpsimd.tensor_copy(idx_src[:, :], src_col[:, bass.ds(2 * g, 2)]).then_inc(idx_ready, 1)

                def gather_x():
                    for u in range(2):
                        pool.indirect_dma_start(out=xe[:, u, :], out_offset=None, in_=x,
                                                in_offset=at(idx_src[:, u:u + 1])).then_inc(xe_gathered, 16)

                source_indices(0)
                waits(pool, "pool", (idx_ready, 1))
                gather_x()

                with pool.Fori(0, PAIRS) as g:
                    source_indices(g + 1)
                    waits(pool, "pool", (table_scattered, 32 * g))
                    nc.gpsimd.tensor_copy(idx_out[:, :], out_col[:, bass.ds(2 * g, 2)]).then_inc(idx_ready, 1)
                    nc.gpsimd.tensor_copy(idx_edge[:, :], edge_col[:, bass.ds(2 * g, 2)]).then_inc(idx_ready, 1)
                    waits(pool, "pool", (idx_ready, 3 * g + 4), (he_ready, g + 1))
                    gather_x()
                    for u in range(2):
                        pool.indirect_dma_start(out=last_edge_of, out_offset=at(idx_out[:, u:u + 1]),
                                                in_=idx_edge[:, u:u + 1], in_offset=None,
                                                bounds_check=N - 1, oob_is_err=False).then_inc(table_scattered, 16)

                def gather_sum1(g):
                    n = g - PAIRS
                    waits(pool, "pool", (table_read, 32 * n), (sum1_gathered, 32 * n))
                    nc.gpsimd.tensor_copy(idx_src[:, :], src_col[:, bass.ds(2 * g, 2)]).then_inc(idx2_ready, 1)
                    waits(pool, "pool", (idx2_ready, n + 1))
                    for u in range(2):
                        pool.indirect_dma_start(out=idx_sum[:, u:u + 1], out_offset=None, in_=last_edge_of,
                                                in_offset=at(idx_src[:, u:u + 1])).then_inc(table_read, 16)
                    waits(pool, "pool", (table_read, 32 * n + 32), (hl1_ready, n))
                    for u in range(2):
                        pool.indirect_dma_start(out=sum1_in[:, u, :], out_offset=None, in_=sum1,
                                                in_offset=at(idx_sum[:, u:u + 1])).then_inc(sum1_gathered, 16)

                waits(pool, "pool", (table_scattered, 32 * PAIRS), (sums_stored, 16 * PAIRS), (xe_gathered, 32 * (PAIRS + 1)))
                gather_sum1(PAIRS)
                with pool.Fori(PAIRS + 1, GROUPS) as g:
                    gather_sum1(g)

            @block.vector
            def _(dve):
                V = nc.vector

                def node_stats(n):
                    waits(dve, "dve", (nroot_ready, 2 * n), (x_loaded, 16 * (n + 1)))
                    x_n = slot(n)
                    for q in range(Q):
                        last = V.bn_stats(nbn[:, q, :], x_n[:, q, :])
                    last.then_inc(nbn_done, 1)
                    waits(dve, "dve", (nbn_done, n + 1))
                    for q in range(Q):
                        last = V.bn_aggr(nmv[:, q, :], nbn[:, q, :])
                    last.then_inc(nstats_ready, 1)

                def edge_stats(n):
                    waits(dve, "dve", (eroot_ready, 2 * n), (xe_gathered, 32 * (n + 1)))
                    for u in range(2):
                        last = V.bn_stats(ebn[:, u, :], xe[:, u, :])
                    last.then_inc(ebn_done, 1)
                    waits(dve, "dve", (ebn_done, n + 1))
                    for u in range(2):
                        last = V.bn_aggr(emv[:, u, :], ebn[:, u, :])
                    last.then_inc(estats_ready, 1)

                def root(n, std_ready, used, used_at, root_ready, rstd, nmr, std, mv):
                    waits(dve, "dve", (std_ready, n + 1), (used, used_at))
                    V.reciprocal(rstd[:, :], std[:, :]).then_inc(root_ready, 1)
                    waits(dve, "dve", (root_ready, 2 * n + 1))
                    V.scalar_tensor_tensor(out=nmr[:, :], in0=mv[:, :, 0], scalar=-1.0, in1=rstd[:, :],
                                           op0=ALU.mult, op1=ALU.mult).then_inc(root_ready, 1)

                def node_root(n):
                    root(n, nstd_ready, hn_ready, n, nroot_ready, nrstd, nnmr, nstd, nmv)

                def edge_root(n):
                    root(n, estd_ready, he_ready, n, eroot_ready, erstd, enmr, estd, emv)

                def product(g, u):
                    h = h_scaled[:, u, :].rearrange("p (b i) -> p b i", i=DB)
                    waits(dve, "dve", (wexp_done, 2 * g + u + 1), (h_ready, g + 1), (msg_ready, 2 * g + u))
                    for half in range(2):
                        b = slice(half * B // 2, (half + 1) * B // 2)
                        last = V.tensor_tensor(
                            prod[:, half * 512:half * 512 + 512].rearrange("p (b o i) -> p b o i", o=DB, i=DB),
                            WX[half][:, :].rearrange("p (b o i) -> p b o i", o=DB, i=DB),
                            h[:, b, :].unsqueeze(2).broadcast_to([P, B // 2, DB, DB]), op=ALU.mult)
                    last.then_inc(prod_done, 1)
                    waits(dve, "dve", (prod_done, 2 * g + u + 1), (agg_done, 2 * g))
                    V.tensor_reduce(out=msg[:, u, :], in_=prod[:, :].rearrange("p (n i) -> p n i", i=DB),
                                    axis=AX.X, op=ALU.add).then_inc(msg_ready, 1)

                def residual(g, a):
                    x_g = slot(g)[:, 2 * a:2 * a + 2, :].rearrange("p q d -> p (q d)")
                    waits(dve, "dve", (mm2_done, 2 * g + a + 1))
                    V.tensor_tensor(x_g, OUT[a][:, :], x_g, op=ALU.add).then_inc(res_ready, 1)

                def masks(g):
                    waits(dve, "dve", (agg_done, 2 * g), (masks_ready, g), (h_ready, g))
                    V.tensor_copy(icols[:, :], inv_col[:, bass.ds(2 * g, 2)])
                    V.tensor_copy(dcols[:, :], dst_col[:, bass.ds(2 * g, 3)]).then_inc(cols_read, 1)
                    waits(dve, "dve", (cols_read, g + 1), (rows_loaded, 16 * (g + 1)))
                    for u in range(2):
                        V.tensor_scalar(onehot[:, u, :], rows[:, u, 1, :], relation_of_part[:, :], None, ALU.is_equal)
                        V.tensor_scalar(carried[:, u, :], rows[:, u, 0, :], dcols[:, u:u + 1], last_part[:, :], ALU.is_equal, ALU.mult)
                        last = V.scalar_tensor_tensor(out=same_dst[:, u, :], in0=rows[:, u, 0, :], scalar=dcols[:, u + 1:u + 2],
                                                      in1=upper[:, :], op0=ALU.is_equal, op1=ALU.mult)
                    last.then_inc(masks_ready, 1)

                def step(g, layer):
                    known = isinstance(g, int)
                    if layer == 1:
                        edge_root(g)
                    masks(g)
                    if layer == 2:
                        n = g - PAIRS
                        waits(dve, "dve", (h_ready, g), (psrc_loaded, 16 * (n + 1)), (sum1_gathered, 32 * (n + 1)))
                        V.tensor_tensor(he[:, :, :], psrc_in[:, :, :], sum1_in[:, :, :], op=ALU.add).then_inc(hl1_ready, 1)
                    if not known or g + 2 < GROUPS:
                        node_stats(g + 2)
                    product(g, 0)
                    residual(g, 0)
                    if not known or g + 2 < GROUPS:
                        node_root(g + 2)
                    product(g, 1)
                    residual(g, 1)
                    if layer == 1:
                        edge_stats(g + 1)

                node_stats(0)
                node_root(0)
                node_stats(1)
                node_root(1)
                edge_stats(0)
                both_loops(dve, step)

            @block.scalar
            def _(act):
                A = nc.scalar.activation

                def node_std(n):
                    waits(act, "act", (nstats_ready, n + 1), (nroot_ready, 2 * n))
                    A(nstd[:, :], nmv[:, :, 1], ACT.Sqrt, bias=eps_col[:, :]).then_inc(nstd_ready, 1)

                def edge_std(n):
                    waits(act, "act", (estats_ready, n + 1), (eroot_ready, 2 * n))
                    A(estd[:, :], emv[:, :, 1], ACT.Sqrt, bias=eps_col[:, :]).then_inc(estd_ready, 1)

                def node_norm(n):
                    waits(act, "act", (nroot_ready, 2 * n + 2), (xT_done, n))
                    x_n = slot(n)
                    for q in range(Q):
                        last = A(hn[:, q, :], x_n[:, q, :], ACT.Relu, scale=nrstd[:, q:q + 1], bias=nnmr[:, q:q + 1])
                    last.then_inc(hn_ready, 1)

                def save_hT(n):
                    waits(act, "act", (xT_done, n + 1), (mm1_done, 2 * n))
                    for a in range(2):
                        last = A(hT[:, :, 2 * a:2 * a + 2, :].rearrange("f k q p -> f q k p"),
                                 XT[a][:, :].rearrange("f (q k p) -> f q k p", q=2, k=K), ACT.Copy)
                    last.then_inc(hT_ready, 1)

                def save_o1(g, m):
                    waits(act, "act", (mm1_done, 2 * g + m + 1), (mm2_done, 2 * g))
                    A(o1T[:, m, :, :].rearrange("f q p -> f (q p)"), P1[m][:, :], ACT.Relu,
                      bias=bias1_col[:, m:m + 1]).then_inc(o1_ready, 1)

                def save_sums(g, u):
                    waits(act, "act", (agg_done, 2 * g + u + 1), (sums_stored, 16 * g))
                    A(sums[:, u, :], XT[u][:, 0:D], ACT.Copy).then_inc(sums_ready, 1)

                def step(g, layer):
                    known = isinstance(g, int)
                    if not known or g + 1 < GROUPS:
                        node_norm(g + 1)
                    if layer == 1:
                        waits(act, "act", (eroot_ready, 2 * g + 2), (eT_done, g), (h_ready, g))
                        for u in range(2):
                            last = A(he[:, u, :], xe[:, u, :], ACT.Relu, scale=erstd[:, u:u + 1], bias=enmr[:, u:u + 1])
                        last.then_inc(he_ready, 1)
                    save_o1(g, 0)
                    waits(act, "act", (he_ready, g + 1) if layer == 1 else (hl1_ready, g - PAIRS + 1),
                          (cols_read, g + 1), (prod_done, 2 * g))
                    for u in range(2):
                        last = A(h_scaled[:, u, :], he[:, u, :], ACT.Relu, scale=icols[:, u:u + 1])
                    last.then_inc(h_ready, 1)
                    save_o1(g, 1)
                    if not known or g + 1 < GROUPS:
                        save_hT(g + 1)
                    if layer == 1:
                        waits(act, "act", (eT_done, g + 1), (eP_done, g))
                        A(hTe[:, :, :, :].rearrange("f u k p -> f (u k p)"), P1[0][:, :], ACT.Copy).then_inc(hTe_ready, 1)
                    if not known or g + 2 < GROUPS:
                        node_std(g + 2)
                    save_sums(g, 0)
                    if layer == 1:
                        waits(act, "act", (eP_done, g + 1), (psrc_stored, 16 * g))
                        A(psrc_out[:, :, :].rearrange("p u d -> p (u d)"), P1[1][:, :], ACT.Copy).then_inc(psrc_ready, 1)
                    save_sums(g, 1)
                    if layer == 1:
                        edge_std(g + 1)

                node_std(0)
                node_norm(0)
                save_hT(0)
                node_std(1)
                edge_std(0)
                both_loops(act, step)

            @block.tensor
            def _(pe):
                mm, T = nc.tensor.matmul, nc.tensor.transpose

                def turn_nodes(n):
                    waits(pe, "pe", (hn_ready, n + 1), (hT_ready, n), (sums_ready, 2 * (n - 1)))
                    for q in range(Q):
                        for k in range(K):
                            at = (q % 2) * D + k * P
                            last = T(XT[q // 2][:, at:at + P], hn[:, q, k * P:(k + 1) * P], ident[:, :])
                    last.then_inc(xT_done, 1)

                def layer_one(g, m):
                    for k in range(K):
                        last = mm(P1[m][:, :], root1_sb[:, k, m * P:(m + 1) * P],
                                  hT[:, k, :, :].rearrange("f q p -> f (q p)"), start=(k == 0), stop=(k == K - 1))
                    last.then_inc(mm1_done, 1)

                def layer_two(g, a):
                    for q in (2 * a, 2 * a + 1):
                        o = OUT[a][:, (q % 2) * D:(q % 2 + 1) * D]
                        mm(o, ones[:, :], bias2_parts[:, :], start=True, stop=False)
                        for k in range(K):
                            last = mm(o, o1T[:, k, q, :], root2_sb[:, k, :], start=False, stop=(k == K - 1))
                    last.then_inc(mm2_done, 1)

                def expand(g, u, layer):
                    for half in range(2):
                        last = mm(WX[half][:, :], onehot[:, u, :], w_parts[layer - 1][:, half * 512:half * 512 + 512],
                                  start=True, stop=True)
                    last.then_inc(wexp_done, 1)

                def aggregate(g, u):
                    waits(pe, "pe", (msg_ready, 2 * g + u + 1), (sums_ready, 2 * g + u))
                    mm(XT[u][:, 0:D], same_dst[:, u, :], msg[:, u, :], start=True, stop=False)
                    mm(XT[u][:, 0:D], carried[:, u, :], sums[:, 1 - u, :], start=False, stop=True).then_inc(agg_done, 1)

                def step(g, layer):
                    known = isinstance(g, int)
                    ahead = not known or g + 1 < GROUPS
                    waits(pe, "pe", (hT_ready, g + 1), (o1_ready, 2 * g),
                          (hTe_ready, g if layer == 1 else PAIRS))
                    layer_one(g, 0)
                    waits(pe, "pe", (psrc_ready, g if layer == 1 else PAIRS))
                    layer_one(g, 1)
                    if ahead:
                        turn_nodes(g + 1)
                    waits(pe, "pe", (masks_ready, g + 1), (prod_done, 2 * g))
                    expand(g, 0, layer)
                    if layer == 1:
                        waits(pe, "pe", (he_ready, g + 1), (o1_ready, 2 * g + 1))
                        for u in range(2):
                            for k in range(K):
                                last = T(P1[0][:, (u * K + k) * P:(u * K + k + 1) * P], he[:, u, k * P:(k + 1) * P], ident[:, :])
                        last.then_inc(eT_done, 1)
                    waits(pe, "pe", (o1_ready, 2 * g + 2), (res_ready, 2 * g))
                    layer_two(g, 0)
                    waits(pe, "pe", (prod_done, 2 * g + 1))
                    expand(g, 1, layer)
                    waits(pe, "pe", (hT_ready, g + 2 if ahead else GROUPS))
                    aggregate(g, 0)
                    layer_two(g, 1)
                    if layer == 1:
                        waits(pe, "pe", (hTe_ready, g + 1))
                        for u in range(2):
                            o = P1[1][:, u * D:(u + 1) * D]
                            mm(o, ones[:, :], bias1_parts[:, :], start=True, stop=False)
                            for k in range(K):
                                last = mm(o, hTe[:, u, k, :], root1_sb[:, k, :], start=False, stop=(k == K - 1))
                        last.then_inc(eP_done, 1)
                    aggregate(g, 1)

                turn_nodes(0)
                both_loops(pe, step)

        xd_gathered = [sem(f"xd_gathered{h}") for h in range(2)]
        s1_loaded = [sem(f"s1_loaded{h}") for h in range(2)]
        s2_loaded = [sem(f"s2_loaded{h}") for h in range(2)]
        fin_scattered = [sem(f"fin_scattered{h}") for h in range(2)]
        idxd_ready, idxf_ready = sem("idxd_ready"), sem("idxf_ready")
        bn3, stats3, std3, root3 = sem("bn3"), sem("stats3"), sem("std3"), sem("root3")
        hn3, resid3, xT3, hT3 = sem("hn3"), sem("resid3"), sem("xT3"), sem("hT3")
        mm3, o3, mm4, fin3 = sem("mm3"), sem("o3"), sem("mm4"), sem("fin3")
        H2 = PAIRS // 2
        assert PAIRS % 2 == 0
        L1 = [bank[2:4], bank[6:8]]

        def in_list(j, ahead):
            return not isinstance(j, int) or 0 <= j + ahead < PAIRS

        def third_loop(eng, step):
            for i in (-1, 0):
                for h in range(2):
                    step(i, h)
            with eng.Fori(1, H2 - 2) as i:
                for h in range(2):
                    step(i, h)
            for i in (H2 - 2, H2 - 1):
                for h in range(2):
                    step(i, h)

        with nc.Block() as block:
            @block.sync
            def _(sp):
                def load1(j, h):
                    sp.dma_start(s1d[:, h, :, :], pair_rows(sum1, j)).then_inc(s1_loaded[h], 16)

                def load2(j, h):
                    sp.dma_start(s2d[:, h, :, :], pair_rows(sum2, j)).then_inc(s2_loaded[h], 16)

                for h in range(2):
                    load1(h, h)
                    load2(h, h)

                def step(i, h):
                    j = 2 * i + h
                    if in_list(j, 3) and not (isinstance(j, int) and j + 3 < 2):
                        waits(sp, "sp", (mm3, j + 2))
                        load1(j + 3, 1 - h)
                    if in_list(j, 4):
                        waits(sp, "sp", (resid3, j + 3))
                        load2(j + 4, h)

                third_loop(sp, step)

            @block.gpsimd
            def _(pool):
                def gather(j, h, n):
                    waits(pool, "pool", (xd_gathered[h], 32 * n), (hn3, j - 1), (resid3, j - 1))
                    nc.gpsimd.tensor_copy(idx_xd[:, h, :], dsti_col[:, bass.ds(2 * j, 2)]).then_inc(idxd_ready, 1)
                    waits(pool, "pool", (idxd_ready, j + 1))
                    for u in range(2):
                        pool.indirect_dma_start(out=xd[:, h, u, :], out_offset=None, in_=x,
                                                in_offset=bass.IndirectOffsetOnAxis(ap=idx_xd[:, h, u:u + 1], axis=0),
                                                bounds_check=N - 1, oob_is_err=False).then_inc(xd_gathered[h], 16)

                def scatter(j, h, i):
                    waits(pool, "pool", (fin_scattered[h], 32 * i))
                    nc.gpsimd.tensor_copy(idx_fin[:, h, :], out_col[:, bass.ds(2 * j, 2)]).then_inc(idxf_ready, 1)
                    waits(pool, "pool", (idxf_ready, j + 1), (fin3, j + 1))
                    for u in range(2):
                        pool.indirect_dma_start(out=out, out_offset=bass.IndirectOffsetOnAxis(ap=idx_fin[:, h, u:u + 1], axis=0),
                                                in_=final[:, h, u, :], in_offset=None,
                                                bounds_check=N - 1, oob_is_err=False).then_inc(fin_scattered[h], 16)

                gather(0, 0, 0)
                gather(1, 1, 0)

                def step(i, h):
                    j = 2 * i + h
                    if in_list(j, 0):
                        scatter(j, h, i)
                    if in_list(j, 4):
                        gather(j + 4, h, i + 2)

                third_loop(pool, step)
                for h in range(2):
                    waits(pool, "pool", (fin_scattered[h], 32 * H2))

            @block.vector
            def _(dve):
                V = nc.vector

                def stats(j, h, n):
                    waits(dve, "dve", (xd_gathered[h], 32 * n), (root3, 2 * j))
                    for u in range(2):
                        last = V.bn_stats(ebn[:, u, :], xd[:, h, u, :])
                    last.then_inc(bn3, 1)
                    waits(dve, "dve", (bn3, j + 1))
                    for u in range(2):
                        last = V.bn_aggr(emv[:, u, :], ebn[:, u, :])
                    last.then_inc(stats3, 1)

                def root(j):
                    waits(dve, "dve", (std3, j + 1), (hn3, j))
                    V.reciprocal(erstd[:, :], estd[:, :]).then_inc(root3, 1)
                    waits(dve, "dve", (root3, 2 * j + 1))
                    V.scalar_tensor_tensor(out=enmr[:, :], in0=emv[:, :, 0], scalar=-1.0, in1=erstd[:, :],
                                           op0=ALU.mult, op1=ALU.mult).then_inc(root3, 1)

                def step(i, h):
                    j = 2 * i + h
                    if in_list(j, 2):
                        root(j + 2)
                    if in_list(j, 0):
                        waits(dve, "dve", (mm4, j + 1), (resid3, j + 1), (fin_scattered[h], 32 * i))
                        V.tensor_tensor(final[:, h, :, :].rearrange("p u d -> p (u d)"), OUT[h][:, :],
                                        resid[:, h, :, :].rearrange("p u d -> p (u d)"), op=ALU.add).then_inc(fin3, 1)
                    if in_list(j, 2):
                        waits(dve, "dve", (xd_gathered[h], 32 * (i + 2)), (s2_loaded[h], 16 * (i + 2)), (fin3, j + 1))
                        V.tensor_tensor(resid[:, h, :, :], xd[:, h, :, :], s2d[:, h, :, :], op=ALU.add).then_inc(resid3, 1)
                    if in_list(j, 3):
                        stats(j + 3, 1 - h, i + 2 + h)

                stats(0, 0, 1)
                third_loop(dve, step)

            @block.scalar
            def _(act):
                A = nc.scalar.activation

                def std_of(j):
                    waits(act, "act", (stats3, j + 1), (root3, 2 * j))
                    A(estd[:, :], emv[:, :, 1], ACT.Sqrt, bias=eps_col[:, :]).then_inc(std3, 1)

                def step(i, h):
                    j = 2 * i + h
                    if in_list(j, 2):
                        waits(act, "act", (root3, 2 * j + 6), (xT3, j + 1))
                        for u in range(2):
                            last = A(hn[:, 2 * h + u, :], xd[:, h, u, :], ACT.Relu, scale=erstd[:, u:u + 1], bias=enmr[:, u:u + 1])
                        last.then_inc(hn3, 1)
                    if in_list(j, 1):
                        waits(act, "act", (mm3, j + 2), (mm4, j))
                        g = 1 - h
                        for m in range(K):
                            last = A(o1T[:, m, 2 * g:2 * g + 2, :].rearrange("f q p -> f (q p)"), L1[g][m][:, 0:2 * P],
                                     ACT.Relu, bias=bias1_col[:, m:m + 1])
                        last.then_inc(o3, 1)
                    if in_list(j, 2):
                        waits(act, "act", (xT3, j + 3), (mm3, j + 1))
                        A(hT[:, :, 2 * h:2 * h + 2, :].rearrange("f k u p -> f u k p"),
                          XT[h][:, :].rearrange("f (u k p) -> f u k p", u=2, k=K), ACT.Copy).then_inc(hT3, 1)
                    if in_list(j, 3):
                        std_of(j + 3)

                std_of(0)
                third_loop(act, step)

            @block.tensor
            def _(pe):
                mm, T = nc.tensor.matmul, nc.tensor.transpose

                def step(i, h):
                    j = 2 * i + h
                    if in_list(j, 1):
                        g = 1 - h
                        waits(pe, "pe", (hT3, j + 2), (s1_loaded[g], 16 * (i + 1 + h)), (o3, j))
                        for m in range(K):
                            for k in range(K):
                                mm(L1[g][m][:, 0:2 * P], root1_sb[:, k, m * P:(m + 1) * P],
                                   hT[:, k, 2 * g:2 * g + 2, :].rearrange("f q p -> f (q p)"), start=(k == 0), stop=False)
                            for u in range(2):
                                last = mm(L1[g][m][:, u * P:(u + 1) * P], s1d[:, g, u, m * P:(m + 1) * P], ident[:, :],
                                          start=False, stop=(u == 1))
                        last.then_inc(mm3, 1)
                    if in_list(j, 2):
                        waits(pe, "pe", (hn3, j + 3), (hT3, j + 1))
                        for u in range(2):
                            for k in range(K):
                                last = T(XT[h][:, u * D + k * P:u * D + (k + 1) * P], hn[:, 2 * h + u, k * P:(k + 1) * P], ident[:, :])
                        last.then_inc(xT3, 1)
                    if in_list(j, 0):
                        waits(pe, "pe", (o3, j + 1), (fin3, j - 1))
                        for u in range(2):
                            o = OUT[h][:, u * D:(u + 1) * D]
                            mm(o, ones[:, :], bias2_parts[:, :], start=True, stop=False)
                            for k in range(K):
                                last = mm(o, o1T[:, k, 2 * h + u, :], root2_sb[:, k, :], start=False, stop=(k == K - 1))
                        last.then_inc(mm4, 1)

                third_loop(pe, step)


_INS = ["x", "src", "dst", "edge_type_16", "L0_gnn_W1", "L0_gnn_root1", "L0_gnn_bias1",
        "L0_gnn_W2", "L0_gnn_root2", "L0_gnn_bias2"]


def kernel(**inputs):
    import numpy as _np
    import concourse.bacc as _bacc
    from concourse import mybir as _mybir
    from concourse.bass_utils import run_bass_kernel_spmd as _run

    nc = _bacc.Bacc("TRN2", target_bir_lowering=False, num_devices=1)
    arrays, args = {}, []
    for name in _INS:
        a = _np.ascontiguousarray(inputs[name])
        arrays[f"in_{name}"] = a
        args.append(nc.dram_tensor(f"in_{name}", a.shape, _mybir.dt.from_np(a.dtype), kind="ExternalInput").ap())
    shape = tuple(inputs["x"].shape)
    args.append(nc.dram_tensor("out_0", shape, _mybir.dt.float32, kind="ExternalOutput").ap())
    build(nc, *args)
    r = _run(nc, [arrays], core_ids=[0])
    return r.results[0]["out_0"]
```

```python
import concourse.bass as bass
import numpy as np
from concourse import mybir
from contextlib import ExitStack

F32, F32R, BF16, I32 = mybir.dt.float32, mybir.dt.float32r, mybir.dt.bfloat16, mybir.dt.int32
ACT, ALU, AX = mybir.ActivationFunctionType, mybir.AluOpType, mybir.AxisListType
P = 128
EPS = 1e-5


def build(nc, x, src, dst, edge_type, w1, root1, bias1, w2, root2, bias2, out):
    N, D = x.shape
    E = src.shape[0]
    R, B, DB, _ = w1.shape
    K = D // P
    Q = 4
    GROUP = Q * P
    COLS = -(-E // P)
    COLS += COLS % 2
    EP = COLS * P
    PAIRS = COLS // 2
    GROUPS = -(-N // GROUP)
    assert GROUPS == 2 * PAIRS and K == 2 and B * DB == D
    LAST_ROW = N - GROUP
    NO_NODE = 1 << 17
    NOT_LAST = 1 << 20
    assert N <= NO_NODE and NO_NODE + NOT_LAST < 1 << 24
    ZERO_ROW = EP
    TABLE = -(-N // P) * P
    W = B * DB * DB

    ctx = ExitStack()
    with ctx:
        def sb(name, shape, dt=F32):
            return ctx.enter_context(nc.sbuf_tensor(name, shape, dt))

        def sem(name):
            return ctx.enter_context(nc.semaphore(name))

        def scratch(name, shape, dt=F32):
            return nc.dram_tensor(name, shape, dt, kind="Internal").ap()

        dst_shifted = scratch("dst_shifted", [EP + 2])
        edge_kinds = scratch("edge_kinds", [5, EP])
        edge_rows = scratch("edge_rows", [2 * COLS, 2, P])
        last_edge_of = scratch("last_edge_of", [TABLE, 1], I32)
        p_src = scratch("p_src", [EP, D])
        sum1 = scratch("sum1", [EP + 1, D])
        sum2 = scratch("sum2", [EP, D])

        ident = sb("ident", [P, P])
        upper = sb("upper", [P, P])
        last_part = sb("last_part", [P, 1])
        ones = sb("ones", [P, P], BF16)
        relation_of_part = sb("relation_of_part", [P, 1])
        eps_col = sb("eps_col", [P, 1])
        root1_sb = sb("root1_sb", [P, K, D])
        root2_sb = sb("root2_sb", [P, K, D])
        bias1_col = sb("bias1_col", [P, K])
        bias1_parts = sb("bias1_parts", [P, D], BF16)
        bias2_parts = sb("bias2_parts", [P, 2 * D], BF16)
        root1_hi, root1_lo = sb("root1_hi", [P, K, D], F32R), sb("root1_lo", [P, K, D], F32R)
        root2_hi, root2_lo = sb("root2_hi", [P, K, D], F32R), sb("root2_lo", [P, K, D], F32R)
        w_parts = [sb(f"w{n}_parts", [P, W], BF16) for n in (1, 2)]
        dst_col = sb("dst_col", [P, 1 + 2 * COLS + 2])
        inv_col = sb("inv_col", [P, 2 * COLS + 2])
        src_col = sb("src_col", [P, 2 * COLS + 2], I32)
        out_col = sb("out_col", [P, COLS], I32)
        edge_col = sb("edge_col", [P, COLS], I32)
        dsti_col = sb("dsti_col", [P, COLS + 4], I32)
        x_sb = sb("x_sb", [P, 4, Q, D])
        nbn, ebn = sb("nbn", [P, Q, 6]), sb("ebn", [P, 2, 6])
        nmv, emv = sb("nmv", [P, Q, 2]), sb("emv", [P, 2, 2])
        nstd, estd = sb("nstd", [P, Q]), sb("estd", [P, 2])
        nrstd, erstd = sb("nrstd", [P, Q]), sb("erstd", [P, 2])
        nnmr, enmr = sb("nnmr", [P, Q]), sb("enmr", [P, 2])
        hn = sb("hn", [P, Q, D])
        hT_hi, hT_lo = sb("hT_hi", [P, K, Q, P], F32R), sb("hT_lo", [P, K, Q, P], F32R)
        o1T = sb("o1T", [P, K, Q, P])
        o1T_hi, o1T_lo = sb("o1T_hi", [P, K, Q, P], F32R), sb("o1T_lo", [P, K, Q, P], F32R)
        xe = sb("xe", [P, 2, D])
        he = sb("he", [P, 2, D])
        hTe = sb("hTe", [P, 2, K, P])
        psrc_out = sb("psrc_out", [P, 2, D])
        psrc_in = sb("psrc_in", [P, 2, D])
        sum1_in = sb("sum1_in", [P, 2, D])
        h_scaled = sb("h_scaled", [P, 2, D])
        rows = sb("rows", [P, 2, 2, 2, P])
        dcols = sb("dcols", [P, 3])
        icols = sb("icols", [P, 2])
        same_dst = sb("same_dst", [P, 2, P])
        carried = sb("carried", [P, 2, P])
        onehot = sb("onehot", [P, 2, P], BF16)
        msg = sb("msg", [P, 2, D])
        sums = sb("sums", [P, 2, D])
        idx_src = sb("idx_src", [P, 2], I32)
        idx_out = sb("idx_out", [P, 2], I32)
        idx_edge = sb("idx_edge", [P, 2], I32)
        idx_sum = sb("idx_sum", [P, 2], I32)
        xd = sb("xd", [P, 4, 2, D])
        idx_xd = sb("idx_xd", [P, 4, 2], I32)
        idx_fin = sb("idx_fin", [P, 4, 2], I32)

        bank = [ctx.enter_context(nc.psum_tensor(f"bank{i}", [P, 512], F32)) for i in range(8)]
        XT, P1, OUT, WX = bank[0:2], bank[2:4], bank[4:6], bank[6:8]

        turn = {e: sem(f"turn_{e}") for e in ("sp", "pool", "dve", "act", "pe")}

        def waits(eng, name, *pairs):
            some = False
            for s, n in pairs:
                if not (isinstance(n, int) and n <= 0):
                    eng.wait_ge(s, n)
                    some = True
            if some:
                eng.sem_inc(turn[name], 1)

        NB = EP // P
        FULL = E // NB
        REST = E - FULL * NB
        with ExitStack() as setup:
            def tb(name, shape, dt=F32):
                return setup.enter_context(nc.sbuf_tensor(name, shape, dt))

            raw = tb("raw", [P, 3, NB], I32)
            kinds = tb("kinds", [P, 5, NB])
            near = tb("near", [P, 2, NB])
            same = tb("same", [P, 2, NB])
            local = tb("local", [P, R, NB])
            onehot_s = tb("onehot_s", [P, R, NB])
            same_rep = tb("same_rep", [P, R, NB])
            run = tb("run", [P, NB])
            count = tb("count", [P, R, NB])
            relation_i = tb("relation_i", [P, R], I32)
            relation_f = tb("relation_f", [P, R])
            end_run = tb("end_run", [P, 2, R])
            carry_t = tb("carry_t", [R, 3, P])
            carry = tb("carry", [P, R])
            minus = tb("minus", [1, 2])
            table0 = tb("table0", [P, TABLE // P], I32)
            zero_row = tb("zero_row", [1, D])
            kind_rows = tb("kind_rows", [P, 2, 5, P])
            part_i = tb("part_i", [P, 1], I32)
            w_f = [tb(f"w{n}_f", [P, W]) for n in (1, 2)]
            w_r = tb("w_r", [P, W])
            b_f = [tb(f"b{n}_f", [P, D]) for n in (1, 2)]
            w_low = tb("w_low", [P, 2, W], BF16)
            back = tb("back", [P, 1])
            flag_row = tb("flag_row", [1, 1])
            flag = tb("flag", [1, 1], I32)
            place = tb("place", [P, R * NB], I32)
            edge_i = tb("edge_i", [P, NB], I32)
            edge_f = tb("edge_f", [P, NB])
            rank = tb("rank", [P, NB])
            rank_i = tb("rank_i", [P, NB], I32)
            of_edge = tb("of_edge", [P, 4])
            rank_col = tb("rank_col", [P, 1], I32)
            payload = tb("payload", [P, 4], I32)
            sorted_in = tb("sorted_in", [P, NB, 4], I32)
            sorted_edges = scratch("sorted_edges", [EP, 4], I32)

            padded = sem("padded")
            edges_in = sem("edges_in")
            consts_in = sem("consts_in")
            pool_consts = sem("pool_consts")
            dst_out = sem("dst_out")
            near_in = sem("near_in")
            kinds_ready = sem("kinds_ready")
            kinds_out = sem("kinds_out")
            kind_rows_in = sem("kind_rows_in")
            rows_out = sem("rows_out")
            table_out = sem("table_out")
            v = sem("setup_dve_step")
            t_done = sem("setup_transposed")
            cols_ready = sem("cols_ready")
            back_ready, back_turned, flag_ready = sem("back_ready"), sem("back_turned"), sem("flag_ready")
            chunk_in, chunk_used = sem("chunk_in"), sem("chunk_used")
            cols_taken, compared, counted, ranked = sem("cols_taken"), sem("compared"), sem("counted"), sem("ranked")
            rank_ready, staged, moved = sem("rank_ready"), sem("staged"), sem("moved")
            all_moved, sorted_ready, unpacked = sem("all_moved"), sem("sorted_ready"), sem("unpacked")
            dst_out2, near_in2 = sem("dst_out2"), sem("near_in2")
            CHUNK = R * NB
            CHUNKS = EP // CHUNK
            assert CHUNKS * CHUNK == EP

            with nc.Block() as block:
                @block.sync
                def _(sp):
                    sp.wait_ge(padded, 1)
                    for k, a in enumerate((dst, edge_type, src)):
                        sp.dma_start(raw[0:FULL, k, :], a[0:FULL * NB].rearrange("(p c) -> p c", c=NB)).then_inc(edges_in, 16)
                        sp.dma_start(raw[FULL:FULL + 1, k, 0:REST], a[FULL * NB:E].rearrange("(p c) -> p c", p=1)).then_inc(edges_in, 16)
                    sp.wait_ge(padded, 2)
                    for n, w in enumerate((w1, w2)):
                        for q in range(3):
                            sp.dma_start(w_f[n][32 * q:32 * q + R, :], w.rearrange("r b i o -> r (b i o)")).then_inc(consts_in, 16)
                    for q in range(3):
                        for n, b in enumerate((bias1, bias2)):
                            sp.dma_start(b_f[n][32 * q:32 * q + 1, :], b.rearrange("(a d) -> a d", a=1)).then_inc(consts_in, 16)
                    sp.dma_start(root1_sb[:, :, :], root1.rearrange("(k p) d -> p k d", p=P)).then_inc(consts_in, 16)
                    sp.dma_start(root2_sb[:, :, :], root2.rearrange("(k p) d -> p k d", p=P)).then_inc(consts_in, 16)
                    with nc.allow_non_contiguous_dma(reason="one column per feature chunk"):
                        sp.dma_start(bias1_col[:, :], bias1.rearrange("(k p) -> p k", p=P)).then_inc(consts_in, 16)
                    sp.wait_ge(kinds_ready, 1)
                    sp.dma_start(dst_shifted[1:EP + 1].rearrange("(p c) -> p c", c=NB), kinds[:, 0, :]).then_inc(dst_out, 16)
                    sp.dma_start(dst_shifted[0:1].rearrange("(p c) -> p c", p=1), minus[:, 0:1]).then_inc(dst_out, 16)
                    sp.dma_start(dst_shifted[EP + 1:EP + 2].rearrange("(p c) -> p c", p=1), minus[:, 1:2]).then_inc(dst_out, 16)
                    sp.wait_ge(dst_out, 48)
                    for k in range(2):
                        sp.dma_start(near[:, k, :], dst_shifted[2 * k:2 * k + EP].rearrange("(p c) -> p c", c=NB)).then_inc(near_in, 16)
                    sp.wait_ge(flag_ready, 1)
                    unsorted = sp.value_load(flag[0:1, 0:1], min_val=0, max_val=1)
                    with sp.If(unsorted > 0):
                        for n in range(CHUNKS):
                            sp.wait_ge(chunk_used, n)
                            sp.dma_start(local[:, :, :].rearrange("p r c -> p (r c)"),
                                         dst_shifted[1 + n * CHUNK:1 + (n + 1) * CHUNK].partition_broadcast(P)).then_inc(chunk_in, 16)
                        sp.wait_ge(all_moved, 1)
                        sp.dma_start(sorted_in[:, :, :], sorted_edges.rearrange("(p c) k -> p c k", c=NB)).then_inc(sorted_ready, 16)
                        sp.wait_ge(unpacked, 1)
                        sp.dma_start(dst_shifted[1:EP + 1].rearrange("(p c) -> p c", c=NB), kinds[:, 0, :]).then_inc(dst_out2, 16)
                        sp.wait_ge(dst_out2, 16)
                        for k in range(2):
                            sp.dma_start(near[:, k, :], dst_shifted[2 * k:2 * k + EP].rearrange("(p c) -> p c", c=NB)).then_inc(near_in2, 16)
                    sp.wait_ge(kinds_ready, 2)
                    sp.dma_start(edge_kinds.rearrange("k (p c) -> p k c", c=NB), kinds[:, :, :]).then_inc(kinds_out, 16)
                    sp.wait_ge(kinds_out, 16)
                    by_tile = edge_kinds.rearrange("k (c p) -> c k p", p=P)
                    sp.dma_start(kind_rows[:, 0, :, :], by_tile[0:P]).then_inc(kind_rows_in, 16)
                    sp.dma_start(kind_rows[0:COLS - P, 1, :, :], by_tile[P:COLS]).then_inc(kind_rows_in, 16)
                    sp.wait_ge(kind_rows_in, 32)
                    for again in (0, COLS):
                        sp.dma_start(edge_rows[again:again + P], kind_rows[:, 0, 0:2, :]).then_inc(rows_out, 16)
                        sp.dma_start(edge_rows[again + P:again + COLS], kind_rows[0:COLS - P, 1, 0:2, :]).then_inc(rows_out, 16)
                    sp.wait_ge(pool_consts, 1)
                    sp.dma_start(last_edge_of.rearrange("(p c) a -> p (c a)", p=P), table0[:, :]).then_inc(table_out, 16)
                    sp.dma_start(sum1[ZERO_ROW:ZERO_ROW + 1, :], zero_row[:, :]).then_inc(table_out, 16)
                    sp.wait_ge(rows_out, 64)
                    sp.wait_ge(table_out, 32)
                    sp.wait_ge(consts_in, 15 * 16)

                @block.gpsimd
                def _(pool):
                    pool.memset(ident[:, :], 0.0).then_inc(turn["pool"], 1)
                    pool.memset(upper[:, :], 1.0).then_inc(turn["pool"], 1)
                    pool.memset(table0[:, :], ZERO_ROW)
                    pool.memset(zero_row[:, :], 0.0)
                    pool.iota(relation_i[:, :], pattern=[[1, R]], base=0, channel_multiplier=0)
                    pool.iota(edge_col[:, :], pattern=[[P, COLS]], base=0, channel_multiplier=1)
                    pool.iota(part_i[:, :], pattern=[[0, 1]], base=0, channel_multiplier=1)
                    pool.iota(place[:, :], pattern=[[1, R * NB]], base=0, channel_multiplier=0)
                    pool.iota(edge_i[:, :], pattern=[[1, NB]], base=0, channel_multiplier=NB)
                    pool.memset(payload[:, :], 0)
                    pool.wait_ge(turn["pool"], 2)
                    pool.affine_select(out=ident[:, :], in_=ident[:, :], compare_op=ALU.not_equal, fill=1.0,
                                       base=0, pattern=[[-1, P]], channel_multiplier=1)
                    pool.affine_select(out=upper[:, :], in_=upper[:, :], compare_op=ALU.is_ge, fill=0.0,
                                       base=0, pattern=[[1, P]], channel_multiplier=-1).then_inc(pool_consts, 1)
                    pool.wait_ge(flag_ready, 1)
                    unsorted = pool.value_load(flag[0:1, 0:1], min_val=0, max_val=1)
                    with pool.If(unsorted > 0):
                        pool.wait_ge(rank_ready, 1)
                        with pool.Fori(0, NB) as c:
                            waits(pool, "pool", (moved, 16 * c))
                            nc.gpsimd.tensor_copy(rank_col[:, :], rank_i[:, bass.ds(c, 1)])
                            nc.gpsimd.tensor_copy(payload[:, 0:3].unsqueeze(2), raw[:, :, bass.ds(c, 1)]).then_inc(staged, 1)
                            waits(pool, "pool", (staged, c + 1))
                            pool.indirect_dma_start(out=sorted_edges, out_offset=bass.IndirectOffsetOnAxis(ap=rank_col[:, :], axis=0),
                                                    in_=payload[:, :], in_offset=None).then_inc(moved, 16)
                        waits(pool, "pool", (moved, 16 * NB))
                        pool.sem_inc(all_moved, 1)

                @block.vector
                def _(dve):
                    step = [0]

                    def do(ins):
                        step[0] += 1
                        ins.then_inc(v, 1)

                    def settle():
                        dve.wait_ge(v, step[0])

                    V = nc.vector
                    do(V.memset(raw[:, 0, :], NO_NODE))
                    settle()
                    V.memset(raw[:, 1:3, :], 0).then_inc(padded, 1)
                    for t in (*w_f, *b_f):
                        do(V.memset(t[:, :], 0.0))
                    do(V.memset(minus[:, :], -1.0))
                    do(V.memset(eps_col[:, :], EPS))
                    do(V.memset(ones[:, :], 1.0))
                    do(V.memset(sums[:, :, :], 0.0))
                    do(V.memset(xd[:, :, :, :], 0.0))
                    do(V.memset(dst_col[:, :], -1.0))
                    do(V.memset(inv_col[:, :], 1.0))
                    do(V.memset(src_col[:, :], 0))
                    do(V.memset(dsti_col[:, :], 0))
                    settle()
                    dve.sem_inc(padded, 1)
                    dve.wait_ge(edges_in, 96)
                    do(V.tensor_copy(kinds[:, 0:3, :], raw[:, :, :]))
                    settle()
                    dve.sem_inc(kinds_ready, 1)
                    dve.wait_ge(pool_consts, 1)
                    do(V.tensor_copy(relation_f[:, :], relation_i[:, :]))
                    for q in range(4):
                        do(V.tensor_scalar(relation_of_part[32 * q:32 * q + 32, :], part_i[32 * q:32 * q + 32, :],
                                           float(-32 * q), None, ALU.add))
                    do(V.tensor_copy(last_part[:, :], ident[:, P - 1:P]))
                    settle()
                    dve.wait_ge(near_in, 32)
                    do(V.tensor_tensor(same[:, 0, :], kinds[:, 0, :], near[:, 0, :], op=ALU.is_lt))
                    settle()
                    do(V.tensor_reduce(out=back[:, :], in_=same[:, 0, :], axis=AX.X, op=ALU.max))
                    settle()
                    dve.sem_inc(back_ready, 1)
                    dve.wait_ge(back_turned, 1)
                    do(V.tensor_reduce(out=flag_row[:, :], in_=bank[1][0:1, 0:P], axis=AX.X, op=ALU.max))
                    settle()
                    do(V.tensor_copy(flag[:, :], flag_row[:, :]))
                    do(V.tensor_copy(edge_f[:, :], edge_i[:, :]))
                    do(V.memset(rank[:, :], 0.0))
                    settle()
                    dve.sem_inc(flag_ready, 1)
                    unsorted = dve.value_load(flag[0:1, 0:1], min_val=0, max_val=1)
                    with dve.If(unsorted > 0):
                        for n in range(CHUNKS):
                            dve.wait_ge(chunk_in, 16 * (n + 1))
                            with dve.Fori(0, NB) as c:
                                t = c + n * NB
                                waits(dve, "dve", (counted, t), (ranked, t))
                                V.tensor_copy(of_edge[:, 0:1], kinds[:, 0, bass.ds(c, 1)])
                                V.tensor_scalar(of_edge[:, 1:2], edge_f[:, bass.ds(c, 1)], float(-n * CHUNK), None,
                                                ALU.add).then_inc(cols_taken, 1)
                                waits(dve, "dve", (cols_taken, t + 1))
                                low = onehot_s[:, :, :].rearrange("p r c -> p (r c)")
                                equal = same_rep[:, :, :].rearrange("p r c -> p (r c)")
                                before = count[:, :, :].rearrange("p r c -> p (r c)")
                                dsts = local[:, :, :].rearrange("p r c -> p (r c)")
                                V.tensor_scalar(low, dsts, of_edge[:, 0:1], None, ALU.is_lt)
                                V.tensor_scalar(equal, dsts, of_edge[:, 0:1], None, ALU.is_equal).then_inc(compared, 1)
                                waits(dve, "dve", (compared, 2 * t + 1))
                                V.scalar_tensor_tensor(out=before, in0=place[:, :], scalar=of_edge[:, 1:2], in1=equal,
                                                       op0=ALU.is_lt, op1=ALU.mult).then_inc(compared, 1)
                                waits(dve, "dve", (compared, 2 * t + 2))
                                V.tensor_reduce(out=of_edge[:, 2:3], in_=low, axis=AX.X, op=ALU.add)
                                V.tensor_reduce(out=of_edge[:, 3:4], in_=before, axis=AX.X, op=ALU.add).then_inc(counted, 1)
                                waits(dve, "dve", (counted, t + 1))
                                V.scalar_tensor_tensor(out=rank[:, bass.ds(c, 1)], in0=of_edge[:, 2:3], scalar=of_edge[:, 3:4],
                                                       in1=rank[:, bass.ds(c, 1)], op0=ALU.add, op1=ALU.add).then_inc(ranked, 1)
                            waits(dve, "dve", (ranked, NB * (n + 1)))
                            dve.sem_inc(chunk_used, 1)
                        V.tensor_copy(rank_i[:, :], rank[:, :]).then_inc(rank_ready, 1)
                        dve.wait_ge(sorted_ready, 16)
                        V.tensor_copy(kinds[:, 0:3, :], sorted_in[:, :, 0:3].rearrange("p c k -> p k c")).then_inc(unpacked, 1)
                        dve.wait_ge(near_in2, 32)
                    do(V.tensor_tensor(onehot_s[:, :, :], kinds[:, 1:2, :].broadcast_to([P, R, NB]),
                                       relation_f[:, :].unsqueeze(2).broadcast_to([P, R, NB]), op=ALU.is_equal))
                    for k in range(2):
                        do(V.tensor_tensor(same[:, k, :], kinds[:, 0, :], near[:, k, :], op=ALU.is_equal))
                    settle()
                    do(V.scalar_tensor_tensor(out=kinds[:, 4, :], in0=same[:, 1, :], scalar=float(NOT_LAST),
                                              in1=kinds[:, 0, :], op0=ALU.mult, op1=ALU.add))
                    for k in range(2):
                        def way(t):
                            return t if k == 0 else t[:, ::-1]
                        first = 0 if k == 0 else NB - 1
                        do(V.tensor_copy(same_rep[:, :, :], same[:, k:k + 1, :].broadcast_to([P, R, NB])))
                        settle()
                        do(V.memset(same_rep[:, :, first:first + 1], 0.0))
                        do(V.tensor_tensor_scan(way(run[:, :]), way(same[:, k, :]), way(same[:, k, :]), 1.0,
                                                op0=ALU.mult, op1=ALU.min))
                        settle()
                        do(V.tensor_tensor_scan(way(local[:, :, :].rearrange("p r c -> p (r c)")),
                                                way(same_rep[:, :, :].rearrange("p r c -> p (r c)")),
                                                way(onehot_s[:, :, :].rearrange("p r c -> p (r c)")), 0.0,
                                                op0=ALU.mult, op1=ALU.add))
                        settle()
                        end = NB - 1 - first
                        do(V.tensor_copy(end_run[:, 0, :], local[:, :, end]))
                        do(V.tensor_copy(end_run[:, 1, :], run[:, end:end + 1].broadcast_to([P, R])))
                        settle()
                        dve.sem_inc(cols_ready, 1)
                        dve.wait_ge(t_done, 1 + 2 * k)
                        do(V.tensor_copy(carry_t[:, 0:2, :], bank[0][0:R, 0:2 * P].rearrange("r (a p) -> r a p", a=2)))
                        settle()
                        do(V.memset(carry_t[:, 2, :], 0.0))
                        settle()
                        if k == 0:
                            do(V.tensor_tensor_scan(carry_t[:, 2, 1:P], carry_t[:, 1, 0:P - 1], carry_t[:, 0, 0:P - 1], 0.0,
                                                    op0=ALU.mult, op1=ALU.add))
                        else:
                            do(V.tensor_tensor_scan(carry_t[:, 2, 0:P - 1][:, ::-1], carry_t[:, 1, 1:P][:, ::-1],
                                                    carry_t[:, 0, 1:P][:, ::-1], 0.0, op0=ALU.mult, op1=ALU.add))
                        settle()
                        dve.sem_inc(cols_ready, 1)
                        dve.wait_ge(t_done, 2 + 2 * k)
                        do(V.tensor_copy(carry[:, :], bank[0][:, 256:256 + R]))
                        settle()
                        do(V.tensor_tensor(same_rep[:, :, :], run[:, :].unsqueeze(1).broadcast_to([P, R, NB]),
                                           carry[:, :].unsqueeze(2).broadcast_to([P, R, NB]), op=ALU.mult))
                        settle()
                        if k == 0:
                            do(V.tensor_tensor(count[:, :, :], local[:, :, :], same_rep[:, :, :], op=ALU.add))
                        else:
                            do(V.tensor_tensor(local[:, :, :], local[:, :, :], same_rep[:, :, :], op=ALU.add))
                            settle()
                            do(V.tensor_tensor(count[:, :, :], count[:, :, :], local[:, :, :], op=ALU.add))
                        settle()
                    do(V.tensor_tensor(count[:, :, :], count[:, :, :], onehot_s[:, :, :], op=ALU.mult))
                    settle()
                    do(V.tensor_reduce(out=run[:, :], in_=count[:, :, :].rearrange("p r c -> p c r"), axis=AX.X, op=ALU.add))
                    settle()
                    do(V.tensor_scalar(run[:, :], run[:, :], -1.0, 1.0, ALU.add, ALU.max))
                    settle()
                    do(V.reciprocal(kinds[:, 3, :], run[:, :]))
                    settle()
                    dve.sem_inc(kinds_ready, 1)
                    dve.wait_ge(consts_in, 15 * 16)
                    for dest, whole, n in ((w_parts[0], w_f[0], W), (w_parts[1], w_f[1], W), (bias1_parts, b_f[0], D),
                                           (bias2_parts, b_f[1], 2 * D)):
                        part = w_low[:, :, 0:n]
                        do(V.memset(dest[:, :], 0.0))
                        if n == W:
                            do(V.tensor_copy(w_r[:, 0:n].rearrange("p (b o i) -> p b o i", o=DB, i=DB),
                                             whole[:, :].rearrange("p (b i o) -> p b o i", o=DB, i=DB)))
                        else:
                            do(V.tensor_copy(w_r[:, 0:n].rearrange("p (a d) -> p a d", d=D),
                                             whole[:, :].unsqueeze(1).broadcast_to([P, n // D, D])))
                        settle()
                        do(V.tensor_copy(dest[:, :], w_r[:, 0:n]))
                        settle()
                        do(V.tensor_tensor(w_r[:, 0:n], w_r[:, 0:n], dest[:, :], op=ALU.subtract))
                        settle()
                        do(V.tensor_copy(part[:, 0, :], w_r[:, 0:n]))
                        settle()
                        do(V.tensor_tensor(w_r[:, 0:n], w_r[:, 0:n], part[:, 0, :], op=ALU.subtract))
                        do(V.tensor_copy(dest[32:64, :], part[32:64, 0, :]))
                        settle()
                        do(V.tensor_copy(dest[64:96, :], w_r[64:96, 0:n]))
                        do(V.memset(dest[96:128, :], 0.0))
                        settle()
                    for whole, hi, lo in ((root1_sb, root1_hi, root1_lo), (root2_sb, root2_hi, root2_lo)):
                        do(V.tensor_copy(hi[:, :, :], whole[:, :, :]))
                        settle()
                        do(V.tensor_tensor(lo[:, :, :], whole[:, :, :], hi[:, :, :].bitcast(F32), op=ALU.subtract))
                    dve.wait_ge(t_done, 5)
                    kind_at = lambda s: bank[2 + s // 2][:, (s % 2) * 256:(s % 2) * 256 + COLS]
                    for again in (0, COLS):
                        do(V.tensor_copy(dst_col[:, 1 + again:1 + again + COLS], kind_at(0)))
                        do(V.tensor_copy(src_col[:, again:again + COLS], kind_at(1)))
                        do(V.tensor_copy(inv_col[:, again:again + COLS], kind_at(2)))
                    do(V.tensor_copy(out_col[:, :], kind_at(3)))
                    do(V.tensor_copy(dsti_col[:, 0:COLS], kind_at(0)))
                    settle()

                @block.tensor
                def _(pe):
                    T = nc.tensor.transpose
                    pe.wait_ge(pool_consts, 1)
                    pe.wait_ge(back_ready, 1)
                    T(bank[1][0:1, 0:P], back[:, :], ident[:, :]).then_inc(back_turned, 1)
                    for k in range(2):
                        pe.wait_ge(cols_ready, 1 + 2 * k)
                        T(bank[0][0:R, 0:P], end_run[:, 0, :], ident[:, :])
                        T(bank[0][0:R, P:2 * P], end_run[:, 1, :], ident[:, :]).then_inc(t_done, 1)
                        pe.wait_ge(cols_ready, 2 + 2 * k)
                        T(bank[0][:, 256:256 + R], carry_t[:, 2, :], ident[0:R, 0:R]).then_inc(t_done, 1)
                    pe.wait_ge(kind_rows_in, 32)
                    for s, k in enumerate((0, 2, 3, 4)):
                        at = (s % 2) * 256
                        T(bank[2 + s // 2][:, at:at + P], kind_rows[:, 0, k, :], ident[:, :])
                        last = T(bank[2 + s // 2][:, at + P:at + COLS], kind_rows[0:COLS - P, 1, k, :],
                                 ident[0:COLS - P, 0:COLS - P])
                    last.then_inc(t_done, 1)

        x_loaded, x_stored = sem("x_loaded"), sem("x_stored")
        nbn_done, nstats_ready, nstd_ready, nroot_ready = sem("nbn_done"), sem("nstats_ready"), sem("nstd_ready"), sem("nroot_ready")
        ebn_done, estats_ready, estd_ready, eroot_ready = sem("ebn_done"), sem("estats_ready"), sem("estd_ready"), sem("eroot_ready")
        hn_ready, xT_done, hT_ready = sem("hn_ready"), sem("xT_done"), sem("hT_ready")
        o1_ready, out1_saved = sem("o1_ready"), sem("out1_saved")
        res1_ready = sem("res1_ready")
        source_ready, onehot_ready = sem("source_ready"), sem("onehot_ready")
        hT_hi_ready, o1_hi_ready, o1_lo_ready = sem("hT_hi_ready"), sem("o1_hi_ready"), sem("o1_lo_ready")
        mm1_done, mm2_done, res_ready = sem("mm1_done"), sem("mm2_done"), sem("res_ready")
        rows_loaded, cols_read, masks_ready = sem("rows_loaded"), sem("cols_read"), sem("masks_ready")
        xe_gathered, table_scattered, idx_ready = sem("xe_gathered"), sem("table_scattered"), sem("idx_ready")
        he_ready, hl1_ready, h_ready = sem("he_ready"), sem("hl1_ready"), sem("h_ready")
        eT_done, hTe_ready, eP_done, psrc_ready = sem("eT_done"), sem("hTe_ready"), sem("eP_done"), sem("psrc_ready")
        psrc_stored, psrc_loaded = sem("psrc_stored"), sem("psrc_loaded")
        wexp_done, prod_done, msg_ready = sem("wexp_done"), sem("prod_done"), sem("msg_ready")
        agg_done, sums_ready, sums_stored = sem("agg_done"), sem("sums_ready"), sem("sums_stored")
        table_read, idx2_ready, sum1_gathered = sem("table_read"), sem("idx2_ready"), sem("sum1_gathered")

        LOOKAHEAD = 3
        PEEL = GROUPS - LOOKAHEAD - 1

        prod = sb("prod", [P, W])
        out1 = sb("out1", [P, 2 * D])

        def nodes_of(t, g):
            start = g * GROUP if not isinstance(g, int) else min(g * GROUP, LAST_ROW)
            return t[bass.ds(start, GROUP), :].rearrange("(p q) d -> p q d", q=Q)

        def slot(g):
            return x_sb[:, bass.ds(g % 4, 1), :, :].rearrange("p a q d -> p (a q) d")

        def pair_rows(t, pair):
            return t[bass.ds(pair * 2 * P, 2 * P), :].rearrange("(u p) d -> p u d", p=P)

        def both_loops(eng, step):
            step(0, 1)
            with eng.Fori(1, PAIRS - 1) as g:
                step(g, 1)
            step(PAIRS - 1, 1)
            step(PAIRS, 2)
            with eng.Fori(PAIRS + 1, PEEL) as g:
                step(g, 2)
            for g in range(PEEL, GROUPS):
                step(g, 2)

        def sums_left(g):
            return not isinstance(g, int) or g not in (0, PAIRS)

        def sums_now(g):
            return isinstance(g, int) and g in (PAIRS - 1, GROUPS - 1)

        def next_edges(g):
            return not isinstance(g, int) or g + 1 < PAIRS

        with nc.Block() as block:
            @block.sync
            def _(sp):
                def load_x(g):
                    sp.dma_start(slot(g), nodes_of(x, g)).then_inc(x_loaded, 16)

                def load_rows(g):
                    sp.dma_start(rows[:, bass.ds(g % 2, 1), :, :, :].rearrange("p a u k e -> p (a u k e)"),
                                 edge_rows[bass.ds(2 * g, 2)].rearrange("u k e -> (u k e)").partition_broadcast(P)
                                 ).then_inc(rows_loaded, 16)

                def load_psrc(pair):
                    sp.dma_start(psrc_in[:, :, :], pair_rows(p_src, pair)).then_inc(psrc_loaded, 16)

                for g in range(LOOKAHEAD):
                    load_x(g)
                    waits(sp, "sp", (x_loaded, 16 * (g + 1)))
                load_rows(0)
                waits(sp, "sp", (rows_loaded, 16))
                load_rows(1)

                def store_sums(g, layer):
                    waits(sp, "sp", (sums_ready, 2 * g + 2))
                    sp.dma_start(pair_rows(sum1 if layer == 1 else sum2, g if layer == 1 else g - PAIRS),
                                 sums[:, :, :]).then_inc(sums_stored, 16)

                def step(g, layer):
                    known = isinstance(g, int)
                    if known and g == PAIRS:
                        waits(sp, "sp", (psrc_stored, 16 * PAIRS))
                        load_psrc(0)
                    if not known or g + LOOKAHEAD < GROUPS:
                        waits(sp, "sp", (x_stored, 16 * g), (x_loaded, 16 * (g + LOOKAHEAD)))
                        load_x(g + LOOKAHEAD)
                    if sums_left(g):
                        store_sums(g - 1, layer)
                    if not known or g + 2 < GROUPS:
                        waits(sp, "sp", (masks_ready, 2 * g + 2), (rows_loaded, 16 * (g + 2)))
                        load_rows(g + 2)
                    if layer == 2 and (not known or g + 1 < GROUPS):
                        waits(sp, "sp", (hl1_ready, g - PAIRS + 1))
                        load_psrc(g + 1 - PAIRS)
                    if known and g == GROUPS - 1:
                        waits(sp, "sp", (x_stored, 16 * g))
                    if layer == 1:
                        waits(sp, "sp", (psrc_ready, g + 1))
                        sp.dma_start(pair_rows(p_src, g), psrc_out[:, :, :]).then_inc(psrc_stored, 16)
                    waits(sp, "sp", (res_ready, g + 1), (res1_ready, g + 1))
                    sp.dma_start(nodes_of(out, g), slot(g)).then_inc(x_stored, 16)
                    if sums_now(g):
                        store_sums(g, layer)

                both_loops(sp, step)
                waits(sp, "sp", (x_stored, 16 * GROUPS), (sums_stored, 16 * GROUPS))

            @block.gpsimd
            def _(pool):
                def at(ap):
                    return bass.IndirectOffsetOnAxis(ap=ap, axis=0)

                def source_indices(g):
                    waits(pool, "pool", (xe_gathered, 32 * g))
                    nc.gpsimd.tensor_copy(idx_src[:, :], src_col[:, bass.ds(2 * g, 2)]).then_inc(source_ready, 1)

                def gather_x():
                    for u in range(2):
                        pool.indirect_dma_start(out=xe[:, u, :], out_offset=None, in_=x,
                                                in_offset=at(idx_src[:, u:u + 1])).then_inc(xe_gathered, 16)

                def low_parts(g):
                    for m in range(K):
                        waits(pool, "pool", (o1_hi_ready, 2 * g + m + 1), (o1_ready, 2 * g + m + 1), (mm2_done, 2 * g))
                        nc.gpsimd.tensor_tensor(o1T_lo[:, m, :, :].rearrange("f q p -> f (q p)"),
                                                o1T[:, m, :, :].rearrange("f q p -> f (q p)"),
                                                o1T_hi[:, m, :, :].bitcast(F32).rearrange("f q p -> f (q p)"),
                                                op=ALU.subtract).then_inc(o1_lo_ready, 1)

                def residual(g):
                    waits(pool, "pool", (out1_saved, g + 1))
                    x_g = slot(g)[:, 2:4, :].rearrange("p q d -> p (q d)")
                    nc.gpsimd.tensor_tensor(x_g, out1[:, :], x_g, op=ALU.add).then_inc(res1_ready, 1)

                source_indices(0)
                waits(pool, "pool", (source_ready, 1))
                gather_x()

                def step1(g):
                    if next_edges(g):
                        source_indices(g + 1)
                        waits(pool, "pool", (source_ready, g + 2), (he_ready, g + 1))
                        gather_x()
                    low_parts(g)
                    waits(pool, "pool", (table_scattered, 32 * g))
                    nc.gpsimd.tensor_copy(idx_out[:, :], out_col[:, bass.ds(2 * g, 2)]).then_inc(idx_ready, 1)
                    nc.gpsimd.tensor_copy(idx_edge[:, :], edge_col[:, bass.ds(2 * g, 2)]).then_inc(idx_ready, 1)
                    waits(pool, "pool", (idx_ready, 2 * g + 2))
                    for u in range(2):
                        pool.indirect_dma_start(out=last_edge_of, out_offset=at(idx_out[:, u:u + 1]),
                                                in_=idx_edge[:, u:u + 1], in_offset=None,
                                                bounds_check=N - 1, oob_is_err=False).then_inc(table_scattered, 16)
                    residual(g)

                with pool.Fori(0, PAIRS - 1) as g:
                    step1(g)
                step1(PAIRS - 1)

                def read_table(g):
                    n = g - PAIRS
                    waits(pool, "pool", (table_read, 32 * n), (sum1_gathered, 32 * n))
                    nc.gpsimd.tensor_copy(idx_src[:, :], src_col[:, bass.ds(2 * g, 2)]).then_inc(idx2_ready, 1)
                    waits(pool, "pool", (idx2_ready, n + 1))
                    for u in range(2):
                        pool.indirect_dma_start(out=idx_sum[:, u:u + 1], out_offset=None, in_=last_edge_of,
                                                in_offset=at(idx_src[:, u:u + 1])).then_inc(table_read, 16)

                def gather_sum1(g):
                    n = g - PAIRS
                    waits(pool, "pool", (table_read, 32 * n + 32), (hl1_ready, n))
                    for u in range(2):
                        pool.indirect_dma_start(out=sum1_in[:, u, :], out_offset=None, in_=sum1,
                                                in_offset=at(idx_sum[:, u:u + 1])).then_inc(sum1_gathered, 16)

                def add_sum1(g):
                    n = g - PAIRS
                    waits(pool, "pool", (psrc_loaded, 16 * (n + 1)), (sum1_gathered, 32 * (n + 1)),
                          (h_ready, g), (eT_done, PAIRS))
                    nc.gpsimd.tensor_tensor(he[:, :, :], psrc_in[:, :, :], sum1_in[:, :, :], op=ALU.add).then_inc(hl1_ready, 1)

                def step2(g):
                    ahead = not isinstance(g, int) or g + 1 < GROUPS
                    if ahead:
                        gather_sum1(g + 1)
                    low_parts(g)
                    if not isinstance(g, int) or g + 2 < GROUPS:
                        read_table(g + 2)
                    residual(g)
                    if ahead:
                        add_sum1(g + 1)

                waits(pool, "pool", (table_scattered, 32 * PAIRS), (sums_stored, 16 * PAIRS), (xe_gathered, 32 * PAIRS))
                read_table(PAIRS)
                gather_sum1(PAIRS)
                read_table(PAIRS + 1)
                add_sum1(PAIRS)
                with pool.Fori(PAIRS, PEEL) as g:
                    step2(g)
                for g in range(PEEL, GROUPS):
                    step2(g)

            @block.vector
            def _(dve):
                V = nc.vector

                def node_stats(n):
                    waits(dve, "dve", (nroot_ready, 2 * n), (x_loaded, 16 * (n + 1)))
                    x_n = slot(n)
                    for q in range(Q):
                        last = V.bn_stats(nbn[:, q, :], x_n[:, q, :])
                    last.then_inc(nbn_done, 1)
                    waits(dve, "dve", (nbn_done, n + 1))
                    for q in range(Q):
                        last = V.bn_aggr(nmv[:, q, :], nbn[:, q, :])
                    last.then_inc(nstats_ready, 1)

                def edge_stats(n):
                    waits(dve, "dve", (eroot_ready, 2 * n), (xe_gathered, 32 * (n + 1)))
                    for u in range(2):
                        last = V.bn_stats(ebn[:, u, :], xe[:, u, :])
                    last.then_inc(ebn_done, 1)
                    waits(dve, "dve", (ebn_done, n + 1))
                    for u in range(2):
                        last = V.bn_aggr(emv[:, u, :], ebn[:, u, :])
                    last.then_inc(estats_ready, 1)

                def root(n, std_ready, used, used_at, root_ready, rstd, nmr, std, mv, between=None):
                    waits(dve, "dve", (std_ready, n + 1), (used, used_at))
                    V.reciprocal(rstd[:, :], std[:, :]).then_inc(root_ready, 1)
                    if between is not None:
                        message(*between)
                    waits(dve, "dve", (root_ready, 2 * n + 1))
                    V.scalar_tensor_tensor(out=nmr[:, :], in0=mv[:, :, 0], scalar=-1.0, in1=rstd[:, :],
                                           op0=ALU.mult, op1=ALU.mult).then_inc(root_ready, 1)

                def node_root(n, between=None):
                    root(n, nstd_ready, hn_ready, n, nroot_ready, nrstd, nnmr, nstd, nmv, between)

                def edge_root(n, between=None):
                    root(n, estd_ready, he_ready, n, eroot_ready, erstd, enmr, estd, emv, between)

                def product(g, u):
                    h = h_scaled[:, u, :].rearrange("p (b i) -> p b i", i=DB)
                    waits(dve, "dve", (wexp_done, 2 * g + u + 1), (h_ready, g + 1), (msg_ready, 2 * g + u))
                    for half in range(2):
                        b = slice(half * B // 2, (half + 1) * B // 2)
                        last = V.tensor_tensor(
                            prod[:, half * 512:half * 512 + 512].rearrange("p (b o i) -> p b o i", o=DB, i=DB),
                            WX[half][:, :].rearrange("p (b o i) -> p b o i", o=DB, i=DB),
                            h[:, b, :].unsqueeze(2).broadcast_to([P, B // 2, DB, DB]), op=ALU.mult)
                    last.then_inc(prod_done, 1)

                def message(g, u):
                    waits(dve, "dve", (prod_done, 2 * g + u + 1), (agg_done, 2 * g))
                    V.tensor_reduce(out=msg[:, u, :], in_=prod[:, :].rearrange("p (n i) -> p n i", i=DB),
                                    axis=AX.X, op=ALU.add).then_inc(msg_ready, 1)

                def low_part(n):
                    waits(dve, "dve", (hT_hi_ready, n + 1), (mm1_done, 2 * n))
                    for a in range(2):
                        last = V.tensor_tensor(hT_lo[:, :, 2 * a:2 * a + 2, :].rearrange("f k q p -> f q k p"),
                                               XT[a][:, :].rearrange("f (q k p) -> f q k p", q=2, k=K),
                                               hT_hi[:, :, 2 * a:2 * a + 2, :].bitcast(F32).rearrange("f k q p -> f q k p"),
                                               op=ALU.subtract)
                    last.then_inc(hT_ready, 1)

                def row(g, tiles, kind):
                    return rows[:, bass.ds(g % 2, 1), tiles, kind, :].rearrange("p a u e -> p (a u) e")

                def relation_mask(g):
                    waits(dve, "dve", (h_ready, g), (masks_ready, 2 * g), (wexp_done, 2 * g))
                    V.tensor_copy(icols[:, :], inv_col[:, bass.ds(2 * g, 2)])
                    V.tensor_copy(dcols[:, :], dst_col[:, bass.ds(2 * g, 3)]).then_inc(cols_read, 1)
                    waits(dve, "dve", (rows_loaded, 16 * (g + 1)))
                    V.tensor_scalar(onehot[:, :, :], row(g, slice(0, 2), 1), relation_of_part[:, :], None, ALU.is_equal).then_inc(onehot_ready, 1)

                def dst_masks(g, u):
                    waits(dve, "dve", (cols_read, g + 1), (agg_done, 2 * g - 1 + u))
                    dst_row = row(g, slice(u, u + 1), 0).rearrange("p u e -> p (u e)")
                    V.tensor_scalar(carried[:, u, :], dst_row, dcols[:, u:u + 1], last_part[:, :], ALU.is_equal, ALU.mult)
                    V.scalar_tensor_tensor(out=same_dst[:, u, :], in0=dst_row, scalar=dcols[:, u + 1:u + 2],
                                           in1=upper[:, :], op0=ALU.is_equal, op1=ALU.mult).then_inc(masks_ready, 1)

                def step(g, layer):
                    known = isinstance(g, int)
                    if not known or g + 2 < GROUPS:
                        node_stats(g + 2)
                    dst_masks(g, 0)
                    product(g, 0)
                    dst_masks(g, 1)
                    if not known or g + 2 < GROUPS:
                        node_root(g + 2, between=(g, 0))
                    else:
                        message(g, 0)
                    if not known or g + 1 < GROUPS:
                        low_part(g + 1)
                    if layer == 1 and next_edges(g):
                        edge_stats(g + 1)
                    product(g, 1)
                    if not known or g + 1 < GROUPS:
                        relation_mask(g + 1)
                    if layer == 1 and next_edges(g):
                        edge_root(g + 1, between=(g, 1))
                    else:
                        message(g, 1)
                    waits(dve, "dve", (mm2_done, 2 * g + 1))
                    x_g = slot(g)[:, 0:2, :].rearrange("p q d -> p (q d)")
                    V.tensor_tensor(x_g, OUT[0][:, :], x_g, op=ALU.add).then_inc(res_ready, 1)

                node_stats(0)
                node_root(0)
                node_stats(1)
                node_root(1)
                edge_stats(0)
                edge_root(0)
                low_part(0)
                relation_mask(0)
                both_loops(dve, step)

            @block.scalar
            def _(act):
                A = nc.scalar.activation

                def node_std(n):
                    waits(act, "act", (nstats_ready, n + 1), (nroot_ready, 2 * n))
                    A(nstd[:, :], nmv[:, :, 1], ACT.Sqrt, bias=eps_col[:, :]).then_inc(nstd_ready, 1)

                def edge_std(n):
                    waits(act, "act", (estats_ready, n + 1), (eroot_ready, 2 * n))
                    A(estd[:, :], emv[:, :, 1], ACT.Sqrt, bias=eps_col[:, :]).then_inc(estd_ready, 1)

                def node_norm(n):
                    waits(act, "act", (nroot_ready, 2 * n + 2), (xT_done, n))
                    x_n = slot(n)
                    for q in range(Q):
                        last = A(hn[:, q, :], x_n[:, q, :], ACT.Relu, scale=nrstd[:, q:q + 1], bias=nnmr[:, q:q + 1])
                    last.then_inc(hn_ready, 1)

                def save_hT(n):
                    waits(act, "act", (xT_done, n + 1), (mm1_done, 2 * n))
                    for a in range(2):
                        last = A(hT_hi[:, :, 2 * a:2 * a + 2, :].rearrange("f k q p -> f q k p"),
                                 XT[a][:, :].rearrange("f (q k p) -> f q k p", q=2, k=K), ACT.Copy)
                    last.then_inc(hT_hi_ready, 1)

                def save_o1(g, m):
                    waits(act, "act", (mm1_done, 2 * g + m + 1), (mm2_done, 2 * g), (o1_lo_ready, 2 * g))
                    for o, ready in ((o1T_hi, o1_hi_ready), (o1T, o1_ready)):
                        A(o[:, m, :, :].rearrange("f q p -> f (q p)"), P1[m][:, :], ACT.Relu,
                          bias=bias1_col[:, m:m + 1]).then_inc(ready, 1)

                def save_sums(g, u):
                    waits(act, "act", (agg_done, 2 * g + u + 1), (sums_stored, 16 * g))
                    A(sums[:, u, :], XT[u][:, 0:D], ACT.Copy).then_inc(sums_ready, 1)

                def edge_norm(n):
                    waits(act, "act", (eroot_ready, 2 * n + 2), (eT_done, n), (h_ready, n))
                    for u in range(2):
                        last = A(he[:, u, :], xe[:, u, :], ACT.Relu, scale=erstd[:, u:u + 1], bias=enmr[:, u:u + 1])
                    last.then_inc(he_ready, 1)

                def step(g, layer):
                    known = isinstance(g, int)
                    save_o1(g, 0)
                    if sums_left(g):
                        save_sums(g - 1, 0)
                    if layer == 1:
                        edge_norm(g)
                    waits(act, "act", (he_ready, g + 1) if layer == 1 else (hl1_ready, g - PAIRS + 1),
                          (cols_read, g + 1), (prod_done, 2 * g))
                    for u in range(2):
                        last = A(h_scaled[:, u, :], he[:, u, :], ACT.Relu, scale=icols[:, u:u + 1])
                    last.then_inc(h_ready, 1)
                    if sums_left(g):
                        save_sums(g - 1, 1)
                    save_o1(g, 1)
                    if not known or g + 2 < GROUPS:
                        node_std(g + 2)
                    if layer == 1:
                        waits(act, "act", (eT_done, g + 1), (eP_done, g))
                        A(hTe[:, :, :, :].rearrange("f u k p -> f (u k p)"), P1[0][:, :], ACT.Copy).then_inc(hTe_ready, 1)
                    if not known or g + 1 < GROUPS:
                        save_hT(g + 1)
                    if not known or g + 2 < GROUPS:
                        node_norm(g + 2)
                    if layer == 1 and next_edges(g):
                        edge_std(g + 1)
                    if layer == 1:
                        waits(act, "act", (eP_done, g + 1), (psrc_stored, 16 * g))
                        A(psrc_out[:, :, :].rearrange("p u d -> p (u d)"), P1[1][:, :], ACT.Copy).then_inc(psrc_ready, 1)
                    waits(act, "act", (mm2_done, 2 * g + 2), (res1_ready, g))
                    A(out1[:, :], OUT[1][:, :], ACT.Copy).then_inc(out1_saved, 1)
                    if sums_now(g):
                        save_sums(g, 0)
                        save_sums(g, 1)

                node_std(0)
                node_norm(0)
                node_std(1)
                node_norm(1)
                edge_std(0)
                save_hT(0)
                both_loops(act, step)

            @block.tensor
            def _(pe):
                mm, T = nc.tensor.matmul, nc.tensor.transpose

                def turn_nodes(n):
                    waits(pe, "pe", (hn_ready, n + 1), (hT_ready, n), (sums_ready, 2 * (n - 1)))
                    for q in range(Q):
                        for k in range(K):
                            at = (q % 2) * D + k * P
                            last = T(XT[q // 2][:, at:at + P], hn[:, q, k * P:(k + 1) * P], ident[:, :])
                    last.then_inc(xT_done, 1)

                def layer_one(g, m):
                    terms = [(k, w, h) for w, h in ((root1_hi, hT_hi), (root1_lo, hT_hi), (root1_hi, hT_lo)) for k in range(K)]
                    for n, (k, w, h) in enumerate(terms):
                        last = mm(P1[m][:, :], w[:, k, m * P:(m + 1) * P], h[:, k, :, :].rearrange("f q p -> f (q p)"),
                                  start=(n == 0), stop=(n == len(terms) - 1))
                    last.then_inc(mm1_done, 1)

                def layer_two(g, a, parts):
                    if 0 in parts:
                        waits(pe, "pe", ((res_ready, out1_saved)[a], g))
                        mm(OUT[a][:, :], ones[:, :], bias2_parts[:, :], start=True, stop=False, skip_group_check=True)
                    for part in parts:
                        o1, w = ((o1T_hi, root2_hi), (o1T_hi, root2_lo), (o1T_lo, root2_hi))[part]
                        for q in (2 * a, 2 * a + 1):
                            for k in range(K):
                                last = mm(OUT[a][:, (q % 2) * D:(q % 2 + 1) * D], o1[:, k, q, :], w[:, k, :],
                                          start=False, stop=(part == 2 and k == K - 1), skip_group_check=True)
                    if 2 in parts:
                        last.then_inc(mm2_done, 1)

                def expand(g, u, layer):
                    for half in range(2):
                        last = mm(WX[half][:, :], onehot[:, u, :], w_parts[layer - 1][:, half * 512:half * 512 + 512],
                                  start=True, stop=True)
                    last.then_inc(wexp_done, 1)

                def aggregate(g, u):
                    waits(pe, "pe", (msg_ready, 2 * g + u + 1), (masks_ready, 2 * g + 2), (sums_ready, 2 * g + u))
                    mm(XT[u][:, 0:D], same_dst[:, u, :], msg[:, u, :], start=True, stop=False)
                    mm(XT[u][:, 0:D], carried[:, u, :], sums[:, 1 - u, :], start=False, stop=True).then_inc(agg_done, 1)

                def step(g, layer):
                    known = isinstance(g, int)
                    ahead = not known or g + 1 < GROUPS
                    waits(pe, "pe", (hT_ready, g + 1), (o1_ready, 2 * g - 1),
                          (hTe_ready, g if layer == 1 else PAIRS))
                    layer_one(g, 0)
                    waits(pe, "pe", (onehot_ready, g + 1), (prod_done, 2 * g))
                    expand(g, 0, layer)
                    if sums_left(g):
                        aggregate(g - 1, 0)
                    waits(pe, "pe", (o1_ready, 2 * g), (psrc_ready, g if layer == 1 else PAIRS))
                    layer_one(g, 1)
                    if sums_left(g):
                        aggregate(g - 1, 1)
                    if layer == 1:
                        waits(pe, "pe", (he_ready, g + 1), (o1_ready, 2 * g + 1))
                        for u in range(2):
                            for k in range(K):
                                last = T(P1[0][:, (u * K + k) * P:(u * K + k + 1) * P], he[:, u, k * P:(k + 1) * P], ident[:, :])
                        last.then_inc(eT_done, 1)
                    if ahead:
                        turn_nodes(g + 1)
                    waits(pe, "pe", (o1_hi_ready, 2 * g + 2))
                    layer_two(g, 0, (0, 1))
                    layer_two(g, 1, (0, 1))
                    waits(pe, "pe", (prod_done, 2 * g + 1))
                    expand(g, 1, layer)
                    if layer == 1:
                        waits(pe, "pe", (hTe_ready, g + 1))
                        for u in range(2):
                            o = P1[1][:, u * D:(u + 1) * D]
                            mm(o, ones[:, :], bias1_parts[:, :], start=True, stop=False)
                            for k in range(K):
                                last = mm(o, hTe[:, u, k, :], root1_sb[:, k, :], start=False, stop=(k == K - 1))
                        last.then_inc(eP_done, 1)
                    waits(pe, "pe", (o1_lo_ready, 2 * g + 2))
                    layer_two(g, 0, (2,))
                    layer_two(g, 1, (2,))
                    if sums_now(g):
                        waits(pe, "pe", (hT_ready, g + 2 if ahead else GROUPS))
                        aggregate(g, 0)
                        aggregate(g, 1)

                turn_nodes(0)
                both_loops(pe, step)

        s1d = sb("s1d", [P, 4, 2, D])
        s2d = sb("s2d", [P, 4, 2, D])
        resid = sb("resid", [P, 4, 2, D])
        final = sb("final", [P, 4, 2, D])
        hTd = sb("hTd", [P, 2, K, 2, P])
        xd_gathered = [sem(f"xd_gathered{r}") for r in range(4)]
        s1_loaded = [sem(f"s1_loaded{r}") for r in range(4)]
        s2_loaded = [sem(f"s2_loaded{r}") for r in range(4)]
        fin_scattered = [sem(f"fin_scattered{r}") for r in range(4)]
        idxd_ready, idxf_ready = sem("idxd_ready"), sem("idxf_ready")
        bn3, stats3, std3, root3 = sem("bn3"), sem("stats3"), sem("std3"), sem("root3")
        hn3, resid3, xT3, hT3 = sem("hn3"), sem("resid3"), sem("xT3"), sem("hT3")
        mm3, o3, mm4, fin3 = sem("mm3"), sem("o3"), sem("mm4"), sem("fin3")
        STEPS = (PAIRS + 2) // 4
        assert STEPS * 4 == PAIRS + 2
        L1 = [bank[2:4], bank[6:8]]

        def in_list(j, ahead):
            return not isinstance(j, int) or 0 <= j + ahead < PAIRS

        def of(i, r, ahead):
            a = r - 2 + ahead
            return a % 4, i + a // 4 + 1

        def third_loop(eng, step):
            for r in range(4):
                step(0, r)
            with eng.Fori(1, STEPS - 2) as i:
                for r in range(4):
                    step(i, r)
            for i in (STEPS - 2, STEPS - 1):
                for r in range(4):
                    step(i, r)

        with nc.Block() as block:
            @block.sync
            def _(sp):
                def load1(j, r):
                    sp.dma_start(s1d[:, r, :, :], pair_rows(sum1, j)).then_inc(s1_loaded[r], 16)

                def load2(j, r):
                    sp.dma_start(s2d[:, r, :, :], pair_rows(sum2, j)).then_inc(s2_loaded[r], 16)

                for j in range(3):
                    load1(j, j)
                    load2(j, j)

                def step(i, r):
                    j = 4 * i - 2 + r
                    if in_list(j, 5):
                        waits(sp, "sp", (mm3, j + 2), (resid3, j + 2))
                        load1(j + 5, of(i, r, 5)[0])
                        load2(j + 5, of(i, r, 5)[0])

                third_loop(sp, step)

            @block.gpsimd
            def _(pool):
                def gather(j, r, n):
                    waits(pool, "pool", (xd_gathered[r], 32 * (n - 1)), (hn3, j - 3), (resid3, j - 3))
                    nc.gpsimd.tensor_copy(idx_xd[:, r, :], dsti_col[:, bass.ds(2 * j, 2)]).then_inc(idxd_ready, 1)
                    waits(pool, "pool", (idxd_ready, j + 1))
                    for u in range(2):
                        pool.indirect_dma_start(out=xd[:, r, u, :], out_offset=None, in_=x,
                                                in_offset=bass.IndirectOffsetOnAxis(ap=idx_xd[:, r, u:u + 1], axis=0),
                                                bounds_check=N - 1, oob_is_err=False).then_inc(xd_gathered[r], 16)

                def scatter(j, r, n):
                    waits(pool, "pool", (fin_scattered[r], 32 * (n - 1)))
                    nc.gpsimd.tensor_copy(idx_fin[:, r, :], out_col[:, bass.ds(2 * j, 2)]).then_inc(idxf_ready, 1)
                    waits(pool, "pool", (idxf_ready, j + 1), (fin3, j + 1))
                    for u in range(2):
                        pool.indirect_dma_start(out=out, out_offset=bass.IndirectOffsetOnAxis(ap=idx_fin[:, r, u:u + 1], axis=0),
                                                in_=final[:, r, u, :], in_offset=None,
                                                bounds_check=N - 1, oob_is_err=False).then_inc(fin_scattered[r], 16)

                for j in range(3):
                    gather(j, j, 1)

                def step(i, r):
                    j = 4 * i - 2 + r
                    if in_list(j, 5):
                        gather(j + 5, *of(i, r, 5))
                    if in_list(j, 0):
                        scatter(j, *of(i, r, 0))

                third_loop(pool, step)
                for r in range(4):
                    waits(pool, "pool", (fin_scattered[r], 32 * len(range(r, PAIRS, 4))))

            @block.vector
            def _(dve):
                V = nc.vector

                def stats(j, r, n):
                    waits(dve, "dve", (xd_gathered[r], 32 * n), (root3, 2 * j))
                    for u in range(2):
                        last = V.bn_stats(ebn[:, u, :], xd[:, r, u, :])
                    last.then_inc(bn3, 1)
                    waits(dve, "dve", (bn3, j + 1))
                    for u in range(2):
                        last = V.bn_aggr(emv[:, u, :], ebn[:, u, :])
                    last.then_inc(stats3, 1)

                def root(j):
                    waits(dve, "dve", (std3, j + 1), (hn3, j))
                    V.reciprocal(erstd[:, :], estd[:, :]).then_inc(root3, 1)
                    waits(dve, "dve", (root3, 2 * j + 1))
                    V.scalar_tensor_tensor(out=enmr[:, :], in0=emv[:, :, 0], scalar=-1.0, in1=erstd[:, :],
                                           op0=ALU.mult, op1=ALU.mult).then_inc(root3, 1)

                def step(i, r):
                    j = 4 * i - 2 + r
                    if in_list(j, 3):
                        stats(j + 3, *of(i, r, 3))
                    if in_list(j, 2):
                        b, n = of(i, r, 2)
                        waits(dve, "dve", (xd_gathered[b], 32 * n), (s2_loaded[b], 16 * n), (fin3, j - 1))
                        V.tensor_tensor(resid[:, b, :, :], xd[:, b, :, :], s2d[:, b, :, :], op=ALU.add).then_inc(resid3, 1)
                    if in_list(j, 3):
                        root(j + 3)
                    if in_list(j, 0):
                        b, n = of(i, r, 0)
                        waits(dve, "dve", (mm4, j + 1), (resid3, j + 1), (fin_scattered[b], 32 * (n - 1)))
                        V.tensor_tensor(final[:, b, :, :].rearrange("p u d -> p (u d)"), OUT[r % 2][:, :],
                                        resid[:, b, :, :].rearrange("p u d -> p (u d)"), op=ALU.add).then_inc(fin3, 1)

                stats(0, 0, 1)
                root(0)
                third_loop(dve, step)

            @block.scalar
            def _(act):
                A = nc.scalar.activation

                def std_of(j):
                    waits(act, "act", (stats3, j + 1), (root3, 2 * j))
                    A(estd[:, :], emv[:, :, 1], ACT.Sqrt, bias=eps_col[:, :]).then_inc(std3, 1)

                def step(i, r):
                    j = 4 * i - 2 + r
                    h = r % 2
                    if in_list(j, 2):
                        waits(act, "act", (root3, 2 * j + 6), (xT3, j + 1))
                        for u in range(2):
                            last = A(hn[:, 2 * h + u, :], xd[:, of(i, r, 2)[0], u, :], ACT.Relu,
                                     scale=erstd[:, u:u + 1], bias=enmr[:, u:u + 1])
                        last.then_inc(hn3, 1)
                    if in_list(j, 3):
                        std_of(j + 3)
                    if in_list(j, 1):
                        waits(act, "act", (mm3, j + 2), (mm4, j))
                        g = 1 - h
                        for m in range(K):
                            last = A(o1T[:, m, 2 * g:2 * g + 2, :].rearrange("f q p -> f (q p)"), L1[g][m][:, 0:2 * P],
                                     ACT.Relu, bias=bias1_col[:, m:m + 1])
                        last.then_inc(o3, 1)
                    if in_list(j, 2):
                        waits(act, "act", (xT3, j + 3), (mm3, j + 1))
                        A(hTd[:, h, :, :, :].rearrange("f k u p -> f u k p"),
                          XT[h][:, :].rearrange("f (u k p) -> f u k p", u=2, k=K), ACT.Copy).then_inc(hT3, 1)

                std_of(0)
                third_loop(act, step)

            @block.tensor
            def _(pe):
                mm, T = nc.tensor.matmul, nc.tensor.transpose

                def step(i, r):
                    j = 4 * i - 2 + r
                    h = r % 2
                    if in_list(j, 1):
                        g = 1 - h
                        b, n = of(i, r, 1)
                        waits(pe, "pe", (hT3, j + 2), (s1_loaded[b], 16 * n), (o3, j))
                        for m in range(K):
                            for k in range(K):
                                mm(L1[g][m][:, 0:2 * P], root1_sb[:, k, m * P:(m + 1) * P],
                                   hTd[:, g, k, :, :].rearrange("f q p -> f (q p)"), start=(k == 0), stop=False)
                            for u in range(2):
                                last = mm(L1[g][m][:, u * P:(u + 1) * P], s1d[:, b, u, m * P:(m + 1) * P], ident[:, :],
                                          start=False, stop=(u == 1))
                        last.then_inc(mm3, 1)
                    if in_list(j, 2):
                        waits(pe, "pe", (hn3, j + 3), (hT3, j + 1))
                        for u in range(2):
                            for k in range(K):
                                last = T(XT[h][:, u * D + k * P:u * D + (k + 1) * P], hn[:, 2 * h + u, k * P:(k + 1) * P], ident[:, :])
                        last.then_inc(xT3, 1)
                    if in_list(j, 0):
                        waits(pe, "pe", (o3, j + 1), (fin3, j - 1))
                        mm(OUT[h][:, :], ones[:, :], bias2_parts[:, :], start=True, stop=False, skip_group_check=True)
                        for u in range(2):
                            for k in range(K):
                                last = mm(OUT[h][:, u * D:(u + 1) * D], o1T[:, k, 2 * h + u, :], root2_sb[:, k, :],
                                          start=False, stop=(k == K - 1), skip_group_check=True)
                        last.then_inc(mm4, 1)

                third_loop(pe, step)


_INS = ["x", "src", "dst", "edge_type_16", "L0_gnn_W1", "L0_gnn_root1", "L0_gnn_bias1",
        "L0_gnn_W2", "L0_gnn_root2", "L0_gnn_bias2"]


def kernel(**inputs):
    import numpy as _np
    import concourse.bacc as _bacc
    from concourse import mybir as _mybir
    from concourse.bass_utils import run_bass_kernel_spmd as _run

    nc = _bacc.Bacc("TRN2", target_bir_lowering=False, num_devices=1)
    arrays, args = {}, []
    for name in _INS:
        a = _np.ascontiguousarray(inputs[name])
        arrays[f"in_{name}"] = a
        args.append(nc.dram_tensor(f"in_{name}", a.shape, _mybir.dt.from_np(a.dtype), kind="ExternalInput").ap())
    shape = tuple(inputs["x"].shape)
    args.append(nc.dram_tensor("out_0", shape, _mybir.dt.float32, kind="ExternalOutput").ap())
    build(nc, *args)
    r = _run(nc, [arrays], core_ids=[0])
    return r.results[0]["out_0"]
```
